# Optimizing a Trainium2 kernel written in Bass

```python
import numpy as np
import jax
import jax.numpy as jnp

def _softmax(x, axis=-1):
    return jax.nn.softmax(x, axis=axis)

def _gelu(x):
    return jax.nn.gelu(x, approximate=True)

def _silu(x):
    return jax.nn.silu(x)

def _sigmoid(x):
    return jax.nn.sigmoid(x)

def _layernorm(x, axis=-1, eps=1e-05):
    m = jnp.mean(x, axis=axis, keepdims=True)
    v = jnp.var(x, axis=axis, keepdims=True)
    return (x - m) / jnp.sqrt(v + eps)

def _scatter_add(tgt, idx, src, axis=0):
    return tgt.at[idx].add(src)

def _segment_sum(src, seg, n):
    return jax.ops.segment_sum(src, seg, n)
kernel_name = 'mk_macaron_d1_jaxref_r8_cf6bf5'

def setup_inputs(seed: int=0):
    np.random.seed(seed)
    _w = jnp.asarray

    def _L0_attn_setup():
        import jax, jax.numpy as jnp
        import numpy as np
        import math
        EMBED_DIM = 256
        NUM_HEADS = 16
        HEAD_DIM = EMBED_DIM // NUM_HEADS
        ROPE_BASE = 10000.0

        def apply_rope(x):
            B, S, H, D = x.shape
            half = D // 2
            positions = jnp.arange(S, dtype=x.dtype)
            inv_freq = 1.0 / ROPE_BASE ** (jnp.arange(0, D, 2, dtype=x.dtype) / D)
            angles = positions[:, None] * inv_freq[None, :]
            sin = jnp.sin(angles)[None, :, None, :]
            cos = jnp.cos(angles)[None, :, None, :]
            x1, x2 = (x[..., :half], x[..., half:])
            return jnp.concatenate([x1 * cos - x2 * sin, x1 * sin + x2 * cos], axis=-1)
        key = jax.random.key(seed)
        ks = jax.random.split(key, 5)
        B, S, E = (2, 256, EMBED_DIM)
        scale = 1.0 / math.sqrt(E)
        return {'x': jax.random.normal(ks[0], (B, S, E), dtype=jnp.float32), 'wq': jax.random.normal(ks[1], (E, E), dtype=jnp.float32) * scale, 'wk': jax.random.normal(ks[2], (E, E), dtype=jnp.float32) * scale, 'wv': jax.random.normal(ks[3], (E, E), dtype=jnp.float32) * scale, 'wo': jax.random.normal(ks[4], (E, E), dtype=jnp.float32) * scale}
    _L0_attn_in = _L0_attn_setup()

    def _L0_ffn_setup():
        import jax, jax.numpy as jnp
        import numpy as np
        D_MODEL = 256
        D_EXPERT = 1024
        EPS = 1e-08

        def ternary_quant(w):
            scale = jnp.mean(jnp.abs(w)) + EPS
            q = jnp.clip(jnp.round(w / scale), -1.0, 1.0) * scale
            return w + jax.lax.stop_gradient(q - w)
        key = jax.random.key(seed)
        k_x, k_up, k_gate, k_down = jax.random.split(key, 4)
        std_in = 1.0 / np.sqrt(D_MODEL)
        std_exp = 1.0 / np.sqrt(D_EXPERT)
        return {'x': jax.random.normal(k_x, (4, 256, D_MODEL), dtype=jnp.float32), 'W_up': jax.random.normal(k_up, (D_EXPERT, D_MODEL), dtype=jnp.float32) * std_in, 'W_gate': jax.random.normal(k_gate, (D_EXPERT, D_MODEL), dtype=jnp.float32) * std_in, 'W_down': jax.random.normal(k_down, (D_MODEL, D_EXPERT), dtype=jnp.float32) * std_exp}
    _L0_ffn_in = _L0_ffn_setup()
    _d = {'L0_attn_x': _L0_attn_in['x'], 'L0_attn_wq': _L0_attn_in['wq'], 'L0_attn_wk': _L0_attn_in['wk'], 'L0_attn_wv': _L0_attn_in['wv'], 'L0_attn_wo': _L0_attn_in['wo'], 'L0_ffn_W_up': _L0_ffn_in['W_up'], 'L0_ffn_W_gate': _L0_ffn_in['W_gate'], 'L0_ffn_W_down': _L0_ffn_in['W_down']}
    _x0 = _d['L0_attn_x']
    _d['L0_attn_x'] = jax.random.normal(jax.random.fold_in(jax.random.key(seed), 1), (16, 256, 256), dtype=_x0.dtype)
    del _x0
    return _d

def reference(L0_attn_x, L0_attn_wq, L0_attn_wk, L0_attn_wv, L0_attn_wo, L0_ffn_W_up, L0_ffn_W_gate, L0_ffn_W_down):

    def _L0_attn_ref(x, wq, wk, wv, wo):
        import jax, jax.numpy as jnp
        import numpy as np
        import math
        EMBED_DIM = 256
        NUM_HEADS = 16
        HEAD_DIM = EMBED_DIM // NUM_HEADS
        ROPE_BASE = 10000.0

        def apply_rope(x):
            B, S, H, D = x.shape
            half = D // 2
            positions = jnp.arange(S, dtype=x.dtype)
            inv_freq = 1.0 / ROPE_BASE ** (jnp.arange(0, D, 2, dtype=x.dtype) / D)
            angles = positions[:, None] * inv_freq[None, :]
            sin = jnp.sin(angles)[None, :, None, :]
            cos = jnp.cos(angles)[None, :, None, :]
            x1, x2 = (x[..., :half], x[..., half:])
            return jnp.concatenate([x1 * cos - x2 * sin, x1 * sin + x2 * cos], axis=-1)
        B, S, E = x.shape
        H, D = (NUM_HEADS, HEAD_DIM)
        q = (x @ wq).reshape(B, S, H, D)
        k = (x @ wk).reshape(B, S, H, D)
        v = (x @ wv).reshape(B, S, H, D)
        q = apply_rope(q)
        k = apply_rope(k)
        scores = jnp.einsum('bqhd,bkhd->bhqk', q, k) / math.sqrt(D)
        causal = jnp.triu(jnp.full((S, S), -jnp.inf, dtype=x.dtype), k=1)
        scores = scores + causal[None, None, :, :]
        attn = jax.nn.softmax(scores, axis=-1)
        out = jnp.einsum('bhqk,bkhd->bqhd', attn, v).reshape(B, S, E)
        return out @ wo

    def _L0_ffn_ref(x, W_up, W_gate, W_down):
        import jax, jax.numpy as jnp
        import numpy as np
        D_MODEL = 256
        D_EXPERT = 1024
        EPS = 1e-08

        def ternary_quant(w):
            scale = jnp.mean(jnp.abs(w)) + EPS
            q = jnp.clip(jnp.round(w / scale), -1.0, 1.0) * scale
            return w + jax.lax.stop_gradient(q - w)
        wu = ternary_quant(W_up)
        wg = ternary_quant(W_gate)
        wd = ternary_quant(W_down)
        up = jnp.einsum('bsd,ed->bse', x, wu)
        gate = jnp.einsum('bsd,ed->bse', x, wg)
        hidden = jax.nn.silu(up) * gate
        return jnp.einsum('bse,de->bsd', hidden, wd)
    x = L0_attn_x
    x = x + 0.5 * _L0_ffn_ref(_layernorm(x, axis=-1), L0_ffn_W_up, L0_ffn_W_gate, L0_ffn_W_down)
    x = x + _L0_attn_ref(_layernorm(x, axis=-1), L0_attn_wq, L0_attn_wk, L0_attn_wv, L0_attn_wo)
    x = x + 0.5 * _L0_ffn_ref(_layernorm(x, axis=-1), L0_ffn_W_up, L0_ffn_W_gate, L0_ffn_W_down)
    return x

_drawn_inputs = setup_inputs


def setup_inputs(seed=0):
    import zlib

    import numpy as np

    out = dict(_drawn_inputs(seed))
    spreads = {}
    factors = {}
    for name, (base, spread) in spreads.items():
        noise = np.random.default_rng([zlib.crc32(name.encode()), seed]).standard_normal(out[name].shape)
        drawn = base * np.exp(spread * noise) if base else spread * noise
        out[name] = jnp.asarray(drawn.astype(out[name].dtype))
    for name, factor in factors.items():
        out[name] = (out[name] * factor).astype(out[name].dtype)
    return out
```

```python
from contextlib import ExitStack

import numpy as np

import concourse.bass as bass
from concourse import mybir

ALU = mybir.AluOpType
ACT = mybir.ActivationFunctionType
AX = mybir.AxisListType
F32 = mybir.dt.float32
F16 = mybir.dt.float16
BF16 = mybir.dt.bfloat16
I32 = mybir.dt.int32
RMAX = bass.bass_isa.ReduceOp.max
RADD = bass.bass_isa.ReduceOp.add

P = 128
NBATCH = 16
SEQ = 256
E = 256
HID = 1024
HEADS = 16
HD = E // HEADS
NT = SEQ // P
NC = E // P
W = NT * E
CHUNKS = HID // P
ROUNDS = CHUNKS // 2
SLOTS = HEADS // 2
STK = 4 * HD
VW = 2 * HD + 1

X_SCALE = 2.0 ** 11
W_SCALE = 2.0 ** 14
Q_SCALE = 2.0 ** 6
QKV_OUT = Q_SCALE / (X_SCALE * W_SCALE)
LN_EPS = 1e-5
QUANT_EPS = 1e-8
MASKED = -1.5 * 2.0 ** 127

MISC = [
    ("norm2", 0, 1), ("qk0", 0, 1), ("qk1", 1, 1), ("attn_t", 2, 3), ("out_proj", 2, 3), ("v", 3, 1),
    ("norm3", 3, 3), ("stack_q0", 4, 1), ("stack_k0", 4, 1), ("stack_q1", 5, 1), ("stack_k1", 5, 1),
    ("norm1", 6, -1),
]
FIRST_STEP = -1
LOOP_FROM, LOOP_TO = 4, 14
LAST_STEP = NBATCH + 3


def live(b):
    return 0 <= b < NBATCH


def misc_before(t, name):
    index = [m[0] for m in MISC].index(name)
    done = sum(live(u - lag) for u in range(FIRST_STEP, t) for _, _, lag in MISC)
    return done + sum(live(t - lag) for _, _, lag in MISC[:index])


def misc_through(t, name):
    return misc_before(t, name) + 1


def rounds_before(t, slot):
    done = sum(ROUNDS * (live(u) + live(u - 3)) for u in range(0, t))
    return done + (min(slot, ROUNDS) * live(t)) + (max(slot - ROUNDS, 0) * live(t - 3))


class Step:

    def __init__(self, first, i=None):
        self.first, self.i = first, i
        self.parity = first % 2

    def live(self, lag):
        return live(self.first - lag)

    def at(self, count, least=1):
        a = count(self.first)
        if self.i is None:
            return max(a, 0)
        slope = count(self.first + 2) - a
        assert count(self.first + 4) - a == 2 * slope and a >= least
        return self.i * slope + a


def run_steps(engine, body, before={}):
    for t in range(FIRST_STEP, LOOP_FROM):
        if t in before:
            before[t]()
        body(Step(t))
    with engine.Fori(0, (LOOP_TO - LOOP_FROM) // 2) as i:
        body(Step(LOOP_FROM, i))
        body(Step(LOOP_FROM + 1, i))
    for t in range(LOOP_TO, LAST_STEP + 1):
        body(Step(t))


def macaron_kernel(nc, x, wqkvo, w_up_t, w_gate_t, w_down_t, ident, mask, rope_cos, rope_sin, out):
    with ExitStack() as ctx:
        def sb(name, shape, dt=F32):
            return ctx.enter_context(nc.sbuf_tensor(name, shape, dt))

        def ps(name, shape, dt=F32):
            return ctx.enter_context(nc.psum_tensor(name, shape, dt))

        def sem(name):
            return ctx.enter_context(nc.semaphore(name))

        ident_f = sb("ident_f", [P, P])
        ident_h = sb("ident_h", [P, P], F16)
        ident_b = sb("ident_b", [P, P], BF16)
        mask_f = sb("mask_f", [P, 2 * P])
        mask_b = sb("mask_b", [P, 2 * P], BF16)
        cos = sb("cos", [P, NT, 2 * E])
        sin = sb("sin", [P, NT, 2 * E])
        raw_up = sb("raw_up", [P, NC * HID])
        raw_gate = sb("raw_gate", [P, NC * HID])
        raw_down = sb("raw_down", [P, CHUNKS * E])
        raw_w = sb("raw_w", [P, NC, 4, E])
        tern_up = sb("tern_up", [P, NC, HID], F16)
        tern_gate = sb("tern_gate", [P, NC, HID], F16)
        tern_down = sb("tern_down", [P, CHUNKS, E], F16)
        below = sb("below", [P, NC * HID], F16)
        w_hi = sb("w_hi", [P, NC, 4, E], F16)
        w_lo = sb("w_lo", [P, NC, 4, E], F16)
        w_absmax = sb("w_absmax", [P, NC * 4])
        w_max = sb("w_max", [P, 4])
        w_max_all = sb("w_max_all", [P, 4])
        w_pow = sb("w_pow", [P, 4])
        w_inv = sb("w_inv", [P, 4])
        w_mul = sb("w_mul", [P, 4])
        abs_sum = sb("abs_sum", [P, 4])
        abs_sum_all = sb("abs_sum_all", [P, 4])
        tern_scale = sb("tern_scale", [P, 4])
        thr_hi = sb("thr_hi", [P, 4])
        thr_lo = sb("thr_lo", [P, 4])
        scale_prod = sb("scale_prod", [P, 4])
        tanh_scale = sb("tanh_scale", [P, 1])
        down_scale = sb("down_scale", [P, 1])
        exp_scale = sb("exp_scale", [P, 1])
        neg_exp_scale = sb("neg_exp_scale", [P, 1])
        proj_scale = sb("proj_scale", [P, 1])
        minus_half = sb("minus_half", [P, NT])

        xs = sb("xs", [P, NBATCH * W])

        stats = {k: sb(f"stats{k}", [P, NT, 6]) for k in (1, 2, 3)}
        mv = {k: sb(f"mv{k}", [P, NT, 2]) for k in (1, 2, 3)}
        var_s = {k: sb(f"var_s{k}", [P, NT]) for k in (1, 2, 3)}
        rstd = {k: sb(f"rstd{k}", [P, NT]) for k in (1, 2, 3)}
        xhat = {k: sb(f"xhat{k}", [P, NT, E]) for k in (1, 2, 3)}
        xt_hi = {k: sb(f"xt_hi{k}", [P, NC, SEQ], F16) for k in (1, 2, 3)}
        xt_lo = {k: sb(f"xt_lo{k}", [P, NC, SEQ], F16) for k in (1, 2, 3)}

        tanh_b = sb("tanh_b", [P, 512])
        silu_b = sb("silu_b", [P, 512])
        hid = sb("hid", [P, 2, 512])
        hid_h = sb("hid_h", [P, 2, 2, SEQ], F16)
        hid_l = sb("hid_l", [P, 2, 2, SEQ], F16)

        rope_c = sb("rope_c", [P, NT, 2 * E])
        rope_s = sb("rope_s", [P, NT, 2 * E])
        rope_r = sb("rope_r", [P, NT, 2 * E])
        q_row = sb("q_row", [P, NT, HEADS, 4, HD], F16)
        k_row = sb("k_row", [P, NT, HEADS, 4, HD], F16)
        q_stk = sb("q_stk", [P, 2, SLOTS, SEQ], F16)
        k_stk = sb("k_stk", [P, 2, SLOTS, SEQ], F16)
        v_row = sb("v_row", [P, 2, NT * HEADS, VW], F16)

        neg_max = sb("neg_max", [P, 4])
        exp_bias = sb("exp_bias", [P, 4])
        prob = sb("prob", [P, 2, 2, 384])
        prob_h = sb("prob_h", [P, 2, 2, 384], F16)
        prob_l = sb("prob_l", [P, 2, 2, 384], F16)
        inv_sum = sb("inv_sum", [P, NT, 2, 1])
        pv_sum = sb("pv_sum", [P, NT, 2, HD])
        attn = sb("attn", [P, NT, E])
        attn_h = sb("attn_h", [P, NC, SEQ], F16)
        attn_l = sb("attn_l", [P, NC, SEQ], F16)

        up_ps = ps("up_ps", [P, 512])
        gate_ps = ps("gate_ps", [P, 512])
        down_ps = ps("down_ps", [P, 512])
        score_ps = ps("score_ps", [P, 2, 512])
        probt_ps = ps("probt_ps", [P, 512])
        pv_ps = ps("pv_ps", [P, 512])
        misc_ps = ps("misc_ps", [P, 512])
        misc_h16 = misc_ps[:, :].bitcast(F16)

        x_loaded = [sem("x_even_loaded"), sem("x_odd_loaded")]
        up_loaded, gate_loaded, down_loaded = sem("up_loaded"), sem("gate_loaded"), sem("down_loaded")
        w_loaded, ident_loaded, mask_loaded = sem("w_loaded"), sem("ident_loaded"), sem("mask_loaded")
        rope_loaded, out_stored = sem("rope_loaded"), sem("out_stored")
        abs_done, abs_all, tern_done = sem("abs_done"), sem("abs_all"), sem("tern_done")
        wmax_done, wmax_all, split_done = sem("wmax_done"), sem("wmax_all"), sem("split_done")
        casts_done, ones_done = sem("casts_done"), sem("ones_done")
        scales_done, w_scales_done = sem("scales_done"), sem("w_scales_done")
        misc_written, scores_done, probt_done = sem("misc_written"), sem("scores_done"), sem("probt_done")
        pv_done, up_done, gate_done = sem("pv_done"), sem("up_done"), sem("gate_done")
        down_done = sem("down_done")
        misc_taken = sem("misc_taken")
        stats_done = {k: sem(f"stats_done{k}") for k in (1, 2, 3)}
        mean_done = {k: sem(f"mean_done{k}") for k in (1, 2, 3)}
        var_done = {k: sem(f"var_done{k}") for k in (1, 2, 3)}
        rstd_done = {k: sem(f"rstd_done{k}") for k in (1, 2, 3)}
        xhat_done = {k: sem(f"xhat_done{k}") for k in (1, 2, 3)}
        xt_hi_done = {k: sem(f"xt_hi_done{k}") for k in (1, 2, 3)}
        tanh_done, silu_done, hid_done = sem("tanh_done"), sem("silu_done"), sem("hid_done")
        hid_h_done, hid_l_done = sem("hid_h_done"), sem("hid_l_done")
        rope_done, row_hi_done, row_lo_done = sem("rope_done"), sem("row_hi_done"), sem("row_lo_done")
        v_hi_done = sem("v_hi_done")
        max_done, bias_done, exp_done = sem("max_done"), sem("bias_done"), sem("exp_done")
        prob_h_done, prob_l_done = sem("prob_h_done"), sem("prob_l_done")
        inv_done, pv_sum_done, attn_done = sem("inv_done"), sem("pv_sum_done"), sem("attn_done")
        attn_h_done = sem("attn_h_done")
        ffn1_added, ffn2_added = sem("ffn1_added"), sem("ffn2_added")

        def x_rows(st, lag, lo=0, n=W):
            return xs[:, bass.ds(st.at(lambda t: (t - lag) * W + lo, least=0), n)]

        x_dram = x.rearrange("b (n p) e -> b p n e", p=P)
        out_dram = out.rearrange("b (n p) e -> b p n e", p=P)

        block = ctx.enter_context(nc.Block())

        @block.sync
        def _(sp):
            def rows(b):
                return xs[:, bass.ds(b * W, W)].rearrange("p (n e) -> p n e", n=NT)

            sp.dma_start(rows(0), x_dram[0]).then_inc(x_loaded[0], 16)
            sp.dma_start(raw_up[:, :], w_up_t).then_inc(up_loaded, 16)
            sp.dma_start(raw_down[:, :], w_down_t).then_inc(down_loaded, 16)
            sp.dma_start(rows(1), x_dram[1]).then_inc(x_loaded[1], 16)
            sp.dma_start(cos[:, :, :], rope_cos).then_inc(rope_loaded, 16)
            sp.dma_start(sin[:, :, :], rope_sin).then_inc(rope_loaded, 16)
            with sp.Fori(1, NBATCH // 2) as i:
                for b in range(2):
                    sp.wait_ge(x_loaded[b], i * 16)
                    sp.dma_start(xs[:, bass.ds(i * (2 * W) + b * W, W)].rearrange("p (n e) -> p n e", n=NT),
                                 x_dram[bass.ds(i * 2 + b, 1)].rearrange("o p n e -> (o p) n e")
                                 ).then_inc(x_loaded[b], 16)
            with sp.Fori(0, NBATCH) as b:
                sp.wait_ge(ffn2_added, b + 1)
                sp.dma_start(out_dram[bass.ds(b, 1)].rearrange("o p n e -> (o p) n e"),
                             xs[:, bass.ds(b * W, W)].rearrange("p (n e) -> p n e", n=NT)
                             ).then_inc(out_stored, 16)
            sp.wait_ge(out_stored, 16 * NBATCH)

        @block.tensor
        def _(pe):
            def split_product(dst, pairs, flags):
                for n, (lhs, rhs) in enumerate(pairs):
                    mm = pe.matmul(dst, lhs, rhs, start=flags and n == 0, stop=n == len(pairs) - 1,
                                   skip_group_check=True)
                return mm

            def three(a_hi, a_lo, b_hi, b_lo):
                return [(a_hi, b_hi), (a_hi, b_lo), (a_lo, b_hi)]

            def scores(st, s):
                pe.wait_ge(misc_taken, st.at(lambda t: misc_through(t - 1, "stack_k1")))
                pe.wait_ge(exp_done, st.at(lambda t: SLOTS * (t - 2) + s))
                par = st.parity
                for j in range(2):
                    pe.matmul(score_ps[:, j, P:3 * P], ident_b[:, :], mask_b[:, :], start=True, stop=False,
                              skip_group_check=True)
                for j in range(2):
                    q = q_stk[STK * j:STK * (j + 1), par, s, :]
                    k = k_stk[STK * j:STK * (j + 1), par, s, :]
                    pe.matmul(score_ps[:, j, 0:2 * P], q[:, P:2 * P], k[:, 0:2 * P], start=False, stop=True,
                              skip_group_check=True)
                    mm = pe.matmul(score_ps[:, j, 2 * P:3 * P], q[:, 0:P], k[:, 0:P], start=False, stop=True,
                                   skip_group_check=True)
                mm.then_inc(scores_done, 1)

            def pair_of(s, back):
                return (2, s - back) if s >= back else (3, s - back + SLOTS)

            def product_v(st, s):
                lag, pair = pair_of(s, 2)
                if not st.live(lag):
                    return
                pe.wait_ge(prob_l_done, st.at(lambda t: 2 * (SLOTS * (t - lag) + pair + 1)))
                pe.wait_ge(pv_sum_done, st.at(lambda t: SLOTS * (t - lag) + pair))
                v = v_row[:, (st.first - lag) % 2, :, :].rearrange("p (n h) w -> p n h w", n=NT)
                first = True
                for j in range(2):
                    h = 2 * pair + j
                    for tile, blocks in ((0, [(0, 0)]), (1, [(1, 0), (2, 1)])):
                        dst = pv_ps[:, (2 * tile + j) * VW:(2 * tile + j + 1) * VW]
                        for col, keys in blocks:
                            for part in (prob_h, prob_l):
                                mm = pe.matmul(dst, part[:, pair % 2, j, col * P:(col + 1) * P], v[:, keys, h, :],
                                               start=first, stop=True, skip_group_check=True)
                                first = False
                mm.then_inc(pv_done, 1)

            def transpose_probs(st, s, j):
                lag, pair = pair_of(s, 1)
                if not st.live(lag):
                    return
                if j == 0:
                    pe.wait_ge(exp_done, st.at(lambda t: SLOTS * (t - lag) + pair + 1))
                pe.wait_ge(prob_l_done, st.at(lambda t: 2 * (SLOTS * (t - lag) + pair) + j))
                for n, col in enumerate((2, 0, 1)):
                    mm = pe.transpose(probt_ps[:, n * P:(n + 1) * P], prob[:, pair % 2, j, col * P:(col + 1) * P],
                                      ident_f[:, :])
                mm.then_inc(probt_done, 1)

            def up_gate(st, s):
                k, lag, r = (1, 0, s) if s < ROUNDS else (3, 3, s - ROUNDS)
                if not st.live(lag):
                    return
                pe.wait_ge(misc_taken, st.at(
                    lambda t: misc_through(t - 1, "norm1") if k == 1 else misc_through(t, "norm3")))
                pe.wait_ge(silu_done, st.at(lambda t: rounds_before(t, s)))
                for dst, tern, done in ((up_ps, tern_up, up_done), (gate_ps, tern_gate, gate_done)):
                    if dst is gate_ps:
                        pe.wait_ge(hid_done, st.at(lambda t: rounds_before(t, s)))
                    for m in range(2):
                        at = (2 * r + m) * P
                        pairs = [(tern[:, c, at:at + P], part[:, c, :]) for c in range(NC)
                                 for part in (xt_hi[k], xt_lo[k])]
                        mm = split_product(dst[:, m * SEQ:(m + 1) * SEQ], pairs, m == 0)
                    mm.then_inc(done, 1)

            def down(st, s):
                lag, r = [(4, 3), (0, 0), (0, 1), (0, 2), (0, 3), (3, 0), (3, 1), (3, 2)][s]
                if not st.live(lag):
                    return
                pe.wait_ge(hid_l_done, st.at(lambda t: rounds_before(t, s)))
                if r == 0:
                    if lag == 0:
                        pe.wait_ge(ffn2_added, st.at(lambda t: t - 3))
                    else:
                        pe.wait_ge(ffn1_added, st.at(lambda t: min(t + 1, NBATCH)))
                par = r % 2
                for tile in range(NT):
                    pairs = [(part[:, par, m, tile * P:(tile + 1) * P], tern_down[:, 2 * r + m, :])
                             for m in range(2) for part in (hid_h, hid_l)]
                    mm = split_product(down_ps[:, tile * E:(tile + 1) * E], pairs, r == 0 and tile == 0)
                mm.then_inc(down_done, 1)

            def transpose_rows(src):
                for c in range(NC):
                    for tile in range(NT):
                        mm = pe.transpose(misc_ps[:, c * SEQ + tile * P:c * SEQ + (tile + 1) * P],
                                          src[:, tile, c * P:(c + 1) * P], ident_f[:, :])
                return mm

            def misc(st, s, half):
                for name, _, lag in [m for m in MISC if m[1] == s][half:half + 1]:
                    if not st.live(lag):
                        continue
                    pe.wait_ge(misc_taken, st.at(lambda t: misc_before(t, name)))
                    if name.startswith("norm"):
                        k = int(name[-1])
                        pe.wait_ge(xhat_done[k], st.at(lambda t: t - lag + 1))
                        mm = transpose_rows(xhat[k])
                    elif name in ("qk0", "qk1"):
                        tile = int(name[-1])
                        pe.wait_ge(split_done, 8)
                        rows = slice(tile * P, (tile + 1) * P)
                        pairs = [p for c in range(NC) for p in three(
                            xt_hi[2][:, c, rows], xt_lo[2][:, c, rows],
                            w_hi[:, c, 0:2, :].rearrange("p m e -> p (m e)"),
                            w_lo[:, c, 0:2, :].rearrange("p m e -> p (m e)"))]
                        mm = split_product(misc_ps[:, :], pairs, True)
                    elif name == "v":
                        for tile in range(NT):
                            rows = slice(tile * P, (tile + 1) * P)
                            pairs = [p for c in range(NC) for p in three(
                                xt_hi[2][:, c, rows], xt_lo[2][:, c, rows], w_hi[:, c, 2, :], w_lo[:, c, 2, :])]
                            mm = split_product(misc_ps[:, tile * E:(tile + 1) * E], pairs, tile == 0)
                    elif name == "attn_t":
                        pe.wait_ge(attn_done, st.at(lambda t: SLOTS * (t - lag + 1)))
                        mm = transpose_rows(attn)
                    elif name == "out_proj":
                        for tile in range(NT):
                            rows = slice(tile * P, (tile + 1) * P)
                            pairs = [p for c in range(NC) for p in three(
                                attn_h[:, c, rows], attn_l[:, c, rows], w_hi[:, c, 3, :], w_lo[:, c, 3, :])]
                            mm = split_product(misc_ps[:, tile * E:(tile + 1) * E], pairs, tile == 0)
                    else:
                        tile = int(name[-1])
                        row = q_row if name.startswith("stack_q") else k_row
                        pe.wait_ge(row_lo_done, st.at(lambda t: 4 * (t - lag) + 2 * tile + (2 if row is k_row else 1)))
                        for pair in range(SLOTS):
                            mm = pe.transpose(misc_h16[:, pair * P:(pair + 1) * P],
                                              row[:, tile, 2 * pair:2 * pair + 2, :, :].rearrange("p h s d -> p (h s d)"),
                                              ident_h[:, :])
                    mm.then_inc(misc_written, 1)

            def step(st):
                for s in range(SLOTS):
                    if st.live(2):
                        scores(st, s)
                    product_v(st, s)
                    misc(st, s, 0)
                    transpose_probs(st, s, 0)
                    up_gate(st, s)
                    transpose_probs(st, s, 1)
                    misc(st, s, 1)
                    down(st, s)

            pe.wait_ge(casts_done, 4)
            pe.wait_ge(ident_loaded, 16)
            run_steps(pe, step, before={0: lambda: pe.wait_ge(tern_done, 3)})

        @block.scalar
        def _(act):
            def set_up_loads():
                act.dma_start(raw_gate[:, :], w_gate_t).then_inc(gate_loaded, 16)
                act.dma_start(ident_f[:, :], ident).then_inc(ident_loaded, 16)
                act.dma_start(mask_f[:, :], mask).then_inc(mask_loaded, 16)
                act.dma_start(raw_w[:, :, :, :], wqkvo).then_inc(w_loaded, 16)

            def set_up():
                for n, (raw, junk, loaded) in enumerate((
                        (raw_up, tern_up, up_loaded), (raw_gate, tern_gate, gate_loaded),
                        (raw_down, tern_down, down_loaded))):
                    act.wait_ge(loaded, 16)
                    act.activation(junk[:, :, :].rearrange("p a b -> p (a b)"), raw[:, :], ACT.Abs,
                                   accum_out=abs_sum[:, n:n + 1]).then_inc(abs_done, 1)
                act.wait_ge(scales_done, 6)

            def split_misc(st, name, lag, dst, done):
                act.wait_ge(misc_written, st.at(lambda t: misc_through(t, name)))
                act.activation(dst[:, :, :].rearrange("p c n -> p (c n)"), misc_ps[:, :], ACT.Copy).then_inc(done, 1)

            def misc(st, s, half):
                for name, _, lag in [m for m in MISC if m[1] == s][half:half + 1]:
                    if not st.live(lag):
                        continue
                    if name.startswith("norm"):
                        k = int(name[-1])
                        split_misc(st, name, lag, xt_hi[k], xt_hi_done[k])
                    elif name == "attn_t":
                        split_misc(st, name, lag, attn_h, attn_h_done)
                    elif name == "v":
                        act.wait_ge(ones_done, 1)
                        act.wait_ge(misc_written, st.at(lambda t: misc_through(t, name)))
                        act.activation(v_row[:, (st.first - lag) % 2, :, 0:HD],
                                       misc_ps[:, :].rearrange("p (m d) -> p m d", d=HD), ACT.Copy,
                                       scale=QKV_OUT).then_inc(v_hi_done, 1)
                    elif name.startswith("stack"):
                        tile = int(name[-1])
                        stk = q_stk if name.startswith("stack_q") else k_stk
                        act.wait_ge(misc_written, st.at(lambda t: misc_through(t, name)))
                        act.activation(stk[:, (st.first - lag) % 2, :, tile * P:(tile + 1) * P],
                                       misc_h16[:, :].rearrange("p (s n) -> p s n", n=P), ACT.Copy
                                       ).then_inc(misc_taken, 1)

            def rope_hi(st, tile):
                if not st.live(1):
                    return
                act.wait_ge(rope_done, st.at(lambda t: 2 * (t - 1) + tile + 1))
                r = rope_r[:, tile, :].rearrange("p (m h d) -> p m h d", m=2, d=HD)
                for m, (row, places) in enumerate(((q_row, slice(0, 4, 3)), (k_row, slice(0, 4, 2)))):
                    dst = row[:, tile, :, places, :]
                    src = r[:, m, :, None, :].to_broadcast([P, HEADS, 2, HD])
                    act.activation(dst, src, ACT.Copy).then_inc(row_hi_done, 1)

            def prob_hi(st, s, j):
                lag, pair = (2, s - 1) if s else (3, SLOTS - 1)
                if not st.live(lag):
                    return
                act.wait_ge(probt_done, st.at(lambda t: 2 * (SLOTS * (t - lag) + pair) + j + 1))
                act.activation(prob_h[:, pair % 2, j, :], probt_ps[:, 0:384], ACT.Copy).then_inc(prob_h_done, 1)

            def exps(st, s):
                act.wait_ge(bias_done, st.at(lambda t: SLOTS * (t - 2) + s + 1))
                for j in range(2):
                    act.activation(prob[:, s % 2, j, 0:256], score_ps[:, j, 0:256], ACT.Exp,
                                   bias=exp_bias[:, j:j + 1], scale=exp_scale[:, :])
                    a = act.activation(prob[:, s % 2, j, 256:384], score_ps[:, j, 256:384], ACT.Exp,
                                       bias=exp_bias[:, 2 + j:3 + j], scale=exp_scale[:, :])
                a.then_inc(exp_done, 1)

            def tanh(st, s):
                if not st.live(0 if s < ROUNDS else 3):
                    return
                act.wait_ge(up_done, st.at(lambda t: rounds_before(t, s) + 1))
                act.activation(tanh_b[:, :], up_ps[:, :], ACT.Tanh, scale=tanh_scale[:, :]).then_inc(tanh_done, 1)

            def hidden_hi(st, s):
                if not st.live(0 if s < ROUNDS else 3):
                    return
                act.wait_ge(hid_done, st.at(lambda t: rounds_before(t, s) + 1))
                act.activation(hid_h[:, s % 2, :, :].rearrange("p m n -> p (m n)"), hid[:, s % 2, :],
                               ACT.Copy).then_inc(hid_h_done, 1)

            def step(st):
                for s in range(SLOTS):
                    misc(st, s, 0)
                    prob_hi(st, s, 0)
                    if st.live(2):
                        exps(st, s)
                    tanh(st, s)
                    prob_hi(st, s, 1)
                    misc(st, s, 1)
                    if s in (1, 2):
                        rope_hi(st, s - 1)
                    hidden_hi(st, s)

            set_up_loads()
            run_steps(act, step, before={0: set_up})

        @block.vector
        def _(dve):
            def set_up_constants():
                dve.memset(minus_half[:, :], -0.5).then_inc(casts_done, 1)
                dve.memset(v_row[:, :, :, 2 * HD:VW], 1.0).then_inc(ones_done, 1)
                dve.wait_ge(ident_loaded, 16)
                dve.tensor_copy(ident_h[:, :], ident_f[:, :]).then_inc(casts_done, 1)
                dve.wait_ge(mask_loaded, 16)
                dve.tensor_copy(mask_b[:, :], mask_f[:, :]).then_inc(casts_done, 1)
                dve.tensor_copy(ident_b[:, :], ident_f[:, :]).then_inc(casts_done, 1)

            def set_up_ternary():
                dve.wait_ge(abs_all, 1)
                dve.tensor_scalar(tern_scale[:, 0:3], abs_sum_all[:, 0:3], 1.0 / (E * HID), QUANT_EPS,
                                  ALU.mult, ALU.add).then_inc(scales_done, 1)
                dve.wait_ge(scales_done, 1)
                dve.tensor_scalar(thr_hi[:, 0:3], tern_scale[:, 0:3], 0.5, None, ALU.mult).then_inc(scales_done, 1)
                dve.tensor_scalar(thr_lo[:, 0:3], tern_scale[:, 0:3], -0.5, None, ALU.mult).then_inc(scales_done, 1)
                dve.tensor_tensor(scale_prod[:, 0:1], tern_scale[:, 0:1], tern_scale[:, 1:2], ALU.mult
                                  ).then_inc(scales_done, 1)
                dve.wait_ge(scales_done, 4)
                dve.tensor_scalar(tanh_scale[:, :], tern_scale[:, 0:1], 0.5 / X_SCALE, None, ALU.mult
                                  ).then_inc(scales_done, 1)
                dve.tensor_tensor(down_scale[:, :], scale_prod[:, 0:1], tern_scale[:, 2:3], ALU.mult
                                  ).then_inc(scales_done, 1)
                for n, (raw, tern) in enumerate(((raw_up, tern_up), (raw_gate, tern_gate), (raw_down, tern_down))):
                    if n:
                        dve.wait_ge(tern_done, n)
                    dve.tensor_scalar(below[:, :], raw[:, :], thr_lo[:, n:n + 1], None, ALU.is_lt
                                      ).then_inc(scales_done, 1)
                    dve.wait_ge(scales_done, 7 + n)
                    dve.scalar_tensor_tensor(out=tern[:, :, :].rearrange("p a b -> p (a b)"), in0=raw[:, :],
                                             scalar=thr_hi[:, n:n + 1], in1=below[:, :], op0=ALU.is_gt,
                                             op1=ALU.subtract).then_inc(tern_done, 1)

            def split_weights():
                dve.wait_ge(w_loaded, 16)
                dve.tensor_reduce(w_absmax[:, :], raw_w[:, :, :, :].rearrange("p c m e -> p (c m) e"), AX.X, ALU.max,
                                  apply_absolute_value=True).then_inc(w_scales_done, 1)
                dve.wait_ge(w_scales_done, 1)
                dve.tensor_tensor(w_max[:, :], w_absmax[:, 0:4], w_absmax[:, 4:8], ALU.max).then_inc(wmax_done, 1)
                dve.wait_ge(wmax_all, 1)
                dve.tensor_scalar(w_max[:, :], w_max_all[:, :], 1e-30, None, ALU.max).then_inc(w_scales_done, 1)
                dve.wait_ge(w_scales_done, 2)
                dve.tensor_scalar(w_pow[:, :].bitcast(I32), w_max[:, :].bitcast(I32), 0x7F800000, None,
                                  ALU.bitwise_and).then_inc(w_scales_done, 1)
                dve.wait_ge(w_scales_done, 3)
                dve.reciprocal(w_inv[:, :], w_pow[:, :]).then_inc(w_scales_done, 1)
                dve.tensor_tensor(scale_prod[:, 1:2], w_pow[:, 0:1], w_pow[:, 1:2], ALU.mult).then_inc(w_scales_done, 1)
                dve.tensor_tensor(scale_prod[:, 2:3], w_pow[:, 2:3], w_pow[:, 3:4], ALU.mult).then_inc(w_scales_done, 1)
                dve.wait_ge(w_scales_done, 6)
                dve.tensor_scalar(w_mul[:, :], w_inv[:, :], W_SCALE, None, ALU.mult).then_inc(w_scales_done, 1)
                to_scores = 1.0 / (Q_SCALE * Q_SCALE * HD ** 0.5)
                dve.tensor_scalar(neg_exp_scale[:, :], scale_prod[:, 1:2], -to_scores, None, ALU.mult
                                  ).then_inc(w_scales_done, 1)
                dve.tensor_scalar(proj_scale[:, :], scale_prod[:, 2:3], 1.0 / (Q_SCALE * W_SCALE), None, ALU.mult
                                  ).then_inc(w_scales_done, 1)
                dve.tensor_scalar(exp_scale[:, :], scale_prod[:, 1:2], to_scores, None, ALU.mult).then_inc(w_scales_done, 1)
                dve.wait_ge(w_scales_done, 10)
                for m in range(4):
                    dve.tensor_scalar(w_hi[:, :, m, :], raw_w[:, :, m, :], w_mul[:, m:m + 1], None, ALU.mult
                                      ).then_inc(split_done, 1)
                for m in range(4):
                    dve.wait_ge(split_done, m + 1)
                    dve.scalar_tensor_tensor(out=w_lo[:, :, m, :], in0=raw_w[:, :, m, :], scalar=w_mul[:, m:m + 1],
                                             in1=w_hi[:, :, m, :], op0=ALU.mult, op1=ALU.subtract
                                             ).then_inc(split_done, 1)
                dve.wait_ge(rope_loaded, 32)

            def wait_norm_rows(st, k, lag):
                if not st.live(lag):
                    return
                if k == 1:
                    dve.wait_ge(x_loaded[(st.first - lag) % 2], st.at(lambda t: 16 * ((t - lag) // 2) + 16))
                elif k == 2:
                    dve.wait_ge(ffn1_added, st.at(lambda t: t - lag + 1))
                else:
                    dve.wait_ge(misc_taken, st.at(lambda t: misc_through(t, "out_proj")))

            def norm_stats(st, k, lag):
                if st.live(lag):
                    for tile in range(NT):
                        dve.bn_stats(stats[k][:, tile, :], x_rows(st, lag, tile * E, E)).then_inc(stats_done[k], 1)

            def wait_stats(st, k, lag):
                if st.live(lag):
                    dve.wait_ge(stats_done[k], st.at(lambda t: 2 * (t - lag + 1)))

            def norm_mean(st, k, lag):
                if st.live(lag):
                    for tile in range(NT):
                        dve.bn_aggr(mv[k][:, tile, :], stats[k][:, tile, :]).then_inc(mean_done[k], 1)

            def norm_var(st, k, lag):
                if st.live(lag):
                    dve.wait_ge(mean_done[k], st.at(lambda t: 2 * (t - lag + 1)))
                    dve.tensor_scalar(var_s[k][:, :, None], mv[k][:, :, 1:2], X_SCALE ** -2, LN_EPS * X_SCALE ** -2,
                                      ALU.mult, ALU.add).then_inc(var_done[k], 1)

            def norm_apply(st, k, lag):
                if not st.live(lag):
                    return
                dve.wait_ge(rstd_done[k], st.at(lambda t: t - lag + 1))
                for tile in range(NT):
                    a = dve.tensor_scalar(xhat[k][:, tile, :], x_rows(st, lag, tile * E, E), mv[k][:, tile, 0:1],
                                          rstd[k][:, tile:tile + 1], ALU.subtract, ALU.mult)
                a.then_inc(xhat_done[k], 1)

            def add_residual(st, src, scale, lag, done):
                rows = x_rows(st, lag)
                return dve.scalar_tensor_tensor(out=rows, in0=src[:, :], scalar=scale[:, :], in1=x_rows(st, lag),
                                                op0=ALU.mult, op1=ALU.add).then_inc(done, 1)

            def ffn_added(st, s):
                lag, done = {1: (4, ffn2_added), 5: (0, ffn1_added)}[s]
                if not st.live(lag):
                    return
                dve.wait_ge(down_done, st.at(lambda t: rounds_before(t, s - 1)))
                add_residual(st, down_ps, down_scale, lag, done)

            def low_part(st, lag, dst, high, hi_done):
                dve.wait_ge(hi_done, st.at(lambda t: t - lag + 1))
                dve.tensor_tensor(dst[:, :, :].rearrange("p c n -> p (c n)"), misc_ps[:, :],
                                  high[:, :, :].rearrange("p c n -> p (c n)"), ALU.subtract).then_inc(misc_taken, 1)

            def misc(st, s, half):
                for name, _, lag in [m for m in MISC if m[1] == s][half:half + 1]:
                    if not st.live(lag):
                        continue
                    if name.startswith("norm"):
                        k = int(name[-1])
                        low_part(st, lag, xt_lo[k], xt_hi[k], xt_hi_done[k])
                    elif name == "attn_t":
                        low_part(st, lag, attn_l, attn_h, attn_h_done)
                    elif name in ("qk0", "qk1"):
                        tile = int(name[-1])
                        dve.wait_ge(misc_written, st.at(lambda t: misc_through(t, name)))
                        dve.tensor_tensor(rope_c[:, tile, :], misc_ps[:, :], cos[:, tile, :], ALU.mult)
                        dve.tensor_tensor(rope_s[:, tile, :], misc_ps[:, :], sin[:, tile, :], ALU.mult
                                          ).then_inc(misc_taken, 1)
                    elif name == "v":
                        v = v_row[:, (st.first - lag) % 2, :, :]
                        dve.wait_ge(v_hi_done, st.at(lambda t: t - lag + 1))
                        dve.scalar_tensor_tensor(out=v[:, :, HD:2 * HD],
                                                 in0=misc_ps[:, :].rearrange("p (m d) -> p m d", d=HD),
                                                 scalar=QKV_OUT, in1=v[:, :, 0:HD], op0=ALU.mult,
                                                 op1=ALU.subtract).then_inc(misc_taken, 1)
                    elif name == "out_proj":
                        dve.wait_ge(misc_written, st.at(lambda t: misc_through(t, name)))
                        add_residual(st, misc_ps, proj_scale, lag, misc_taken)

            def row_max(st, s):
                dve.wait_ge(scores_done, st.at(lambda t: SLOTS * (t - 2) + s + 1))
                dve.tensor_reduce(neg_max[:, 0:2], score_ps[:, :, 0:256], AX.X, ALU.max, negate=True)
                dve.tensor_reduce(neg_max[:, 2:4], score_ps[:, :, 256:384], AX.X, ALU.max, negate=True
                                  ).then_inc(max_done, 1)

            def exp_biases(st, s):
                dve.wait_ge(max_done, st.at(lambda t: SLOTS * (t - 2) + s + 1))
                dve.tensor_scalar(exp_bias[:, :], neg_max[:, :], exp_scale[:, :], None, ALU.mult
                                  ).then_inc(bias_done, 1)

            def pv_parts(s):
                return (2, s - 2) if s >= 2 else (3, s - 2 + SLOTS)

            pv = pv_ps[:, 0:4 * VW].rearrange("p (n j w) -> p n j w", n=NT, j=2)

            def pv_inverse(st, s):
                lag, pair = pv_parts(s)
                if st.live(lag):
                    dve.wait_ge(pv_done, st.at(lambda t: SLOTS * (t - lag) + pair + 1))
                    dve.reciprocal(inv_sum[:, :, :, :], pv[:, :, :, 2 * HD:VW]).then_inc(inv_done, 1)

            def pv_add(st, s):
                lag, pair = pv_parts(s)
                if st.live(lag):
                    dve.wait_ge(pv_done, st.at(lambda t: SLOTS * (t - lag) + pair + 1))
                    dve.tensor_reduce(pv_sum[:, :, :, :].rearrange("p n j d -> p (n j) d"),
                                      pv_ps[:, 0:4 * VW].rearrange("p (m w) -> p m w", w=VW)[:, :, 0:2 * HD]
                                      .rearrange("p m (a d) -> p m d a", a=2), AX.X, ALU.add
                                      ).then_inc(pv_sum_done, 1)

            def pv_scale(st, s):
                lag, pair = pv_parts(s)
                if st.live(lag):
                    if pair == 0:
                        dve.wait_ge(attn_h_done, st.at(lambda t: t - lag))
                    dve.wait_ge(inv_done, st.at(lambda t: SLOTS * (t - lag) + pair + 1))
                    dve.wait_ge(pv_sum_done, st.at(lambda t: SLOTS * (t - lag) + pair + 1))
                    dve.tensor_tensor(attn[:, :, 2 * pair * HD:2 * (pair + 1) * HD]
                                      .rearrange("p n (j d) -> p n j d", j=2), pv_sum[:, :, :, :],
                                      inv_sum[:, :, :, :].to_broadcast([P, NT, 2, HD]), ALU.mult
                                      ).then_inc(attn_done, 1)

            def prob_lo(st, s, j):
                lag, pair = (2, s - 1) if s else (3, SLOTS - 1)
                if not st.live(lag):
                    return
                dve.wait_ge(prob_h_done, st.at(lambda t: 2 * (SLOTS * (t - lag) + pair) + j + 1))
                dve.tensor_tensor(prob_l[:, pair % 2, j, :], probt_ps[:, 0:384], prob_h[:, pair % 2, j, :],
                                  ALU.subtract).then_inc(prob_l_done, 1)

            def silu(st, s):
                if not st.live(0 if s < ROUNDS else 3):
                    return
                dve.wait_ge(tanh_done, st.at(lambda t: rounds_before(t, s) + 1))
                dve.scalar_tensor_tensor(out=silu_b[:, :], in0=tanh_b[:, :], scalar=1.0, in1=up_ps[:, :],
                                         op0=ALU.add, op1=ALU.mult).then_inc(silu_done, 1)

            def hidden(st, s):
                if not st.live(0 if s < ROUNDS else 3):
                    return
                dve.wait_ge(hid_l_done, st.at(lambda t: rounds_before(t, s) - 1))
                dve.wait_ge(gate_done, st.at(lambda t: rounds_before(t, s) + 1))
                dve.wait_ge(silu_done, st.at(lambda t: rounds_before(t, s) + 1))
                dve.scalar_tensor_tensor(out=hid[:, s % 2, :], in0=silu_b[:, :], scalar=0.25 / X_SCALE ** 2,
                                         in1=gate_ps[:, :], op0=ALU.mult, op1=ALU.mult).then_inc(hid_done, 1)

            norm_at = {3: (3, 3), 4: (1, -1), 6: (2, 0)}
            apply_at = {3: (3, 3), 5: (1, -1), 7: (2, 0)}

            def step(st):
                for s in range(SLOTS):
                    norm = norm_at.get(s)
                    if st.live(2):
                        row_max(st, s)
                    pv_inverse(st, s)
                    if s in (1, 5):
                        ffn_added(st, s)
                    if norm:
                        wait_norm_rows(st, *norm)
                    if st.live(2):
                        exp_biases(st, s)
                    if norm:
                        norm_stats(st, *norm)
                        wait_stats(st, *norm)
                    pv_add(st, s)
                    if norm:
                        norm_mean(st, *norm)
                    misc(st, s, 0)
                    if norm:
                        norm_var(st, *norm)
                    pv_scale(st, s)
                    prob_lo(st, s, 0)
                    silu(st, s)
                    if s in apply_at:
                        norm_apply(st, *apply_at[s])
                    prob_lo(st, s, 1)
                    hidden(st, s)
                    misc(st, s, 1)

            set_up_constants()
            run_steps(dve, step, before={0: set_up_ternary, 1: split_weights})

        @block.gpsimd
        def _(pool):
            def rstd_power(st, k, lag):
                if not st.live(lag):
                    return
                pool.wait_ge(var_done[k], st.at(lambda t: t - lag + 1))
                pool.tensor_tensor(rstd[k][:, :], var_s[k][:, :], minus_half[:, :], ALU.pow).then_inc(rstd_done[k], 1)

            def rope_add(st, tile):
                if not st.live(1):
                    return
                pool.wait_ge(misc_taken, st.at(lambda t: misc_through(t, f"qk{tile}")))

                def halves(a):
                    return a[:, tile, :].rearrange("p (h a d) -> p h a d", a=2, d=HD // 2)

                pool.tensor_tensor(halves(rope_r), halves(rope_c), halves(rope_s)[:, :, ::-1, :], ALU.add
                                   ).then_inc(rope_done, 1)

            def row_lo(st, tile, m):
                if not st.live(1):
                    return
                row, places = ((q_row, slice(1, 3)), (k_row, slice(1, 4, 2)))[m]
                r = rope_r[:, tile, :].rearrange("p (m h d) -> p m h d", m=2, d=HD)[:, m]
                pool.wait_ge(row_hi_done, st.at(lambda t: 4 * (t - 1) + 2 * tile + m + 1))
                pool.tensor_tensor(row[:, tile, :, places, :], r[:, :, None, :].to_broadcast([P, HEADS, 2, HD]),
                                   row[:, tile, :, 0:1, :].to_broadcast([P, HEADS, 2, HD]), ALU.subtract
                                   ).then_inc(row_lo_done, 1)

            def hidden_lo(st, s):
                if not st.live(0 if s < ROUNDS else 3):
                    return
                pool.wait_ge(hid_h_done, st.at(lambda t: rounds_before(t, s) + 1))
                pool.tensor_tensor(hid_l[:, s % 2, :, :].rearrange("p m n -> p (m n)"), hid[:, s % 2, :],
                                   hid_h[:, s % 2, :, :].rearrange("p m n -> p (m n)"), ALU.subtract
                                   ).then_inc(hid_l_done, 1)

            def step(st):
                for s in range(SLOTS):
                    if s == 1:
                        rope_add(st, 0)
                    if s == 2:
                        row_lo(st, 0, 0)
                        rope_add(st, 1)
                    if s == 3:
                        rstd_power(st, 3, 3)
                        row_lo(st, 0, 1)
                        row_lo(st, 1, 0)
                    if s == 4:
                        row_lo(st, 1, 1)
                        rstd_power(st, 1, -1)
                    if s == 6:
                        rstd_power(st, 2, 0)
                    hidden_lo(st, s)

            def sum_all():
                pool.wait_ge(abs_done, 3)
                pool.partition_all_reduce(abs_sum_all[:, 0:3], abs_sum[:, 0:3], P, RADD).then_inc(abs_all, 1)

            def max_all():
                pool.wait_ge(wmax_done, 1)
                pool.partition_all_reduce(w_max_all[:, :], w_max[:, :], P, RMAX).then_inc(wmax_all, 1)

            pool.wait_ge(casts_done, 1)
            run_steps(pool, step, before={0: sum_all, 1: max_all})


def kernel(L0_attn_x, L0_attn_wq, L0_attn_wk, L0_attn_wv, L0_attn_wo, L0_ffn_W_up, L0_ffn_W_gate, L0_ffn_W_down):
    import concourse.bacc as bacc
    from concourse.bass_utils import run_bass_kernel_spmd

    def rows_to_partitions(a):
        a = np.ascontiguousarray(a)
        return np.ascontiguousarray(a.reshape(a.shape[0] // P, P, a.shape[1]).transpose(1, 0, 2).reshape(P, -1))

    wqkvo = np.stack([rows_to_partitions(w).reshape(P, NC, E)
                      for w in (L0_attn_wq, L0_attn_wk, L0_attn_wv, L0_attn_wo)], axis=2)

    freq = (1.0 / np.float32(10000.0) ** (np.arange(0, HD, 2, dtype=np.float32) / np.float32(HD))).astype(np.float32)
    angle = np.arange(SEQ, dtype=np.float32)[:, None] * freq[None, :]
    s, c = np.sin(angle) * np.float32(QKV_OUT), np.cos(angle) * np.float32(QKV_OUT)

    def table(first_half, second_half):
        head = np.concatenate([first_half, second_half], axis=1).astype(np.float32)
        return np.ascontiguousarray(np.tile(head, (1, 2 * HEADS)).reshape(NT, P, 2 * E).transpose(1, 0, 2))

    future = np.triu(np.full((P, P), MASKED, dtype=np.float32), k=1)
    arrays = {
        "x": np.ascontiguousarray(L0_attn_x),
        "wqkvo": np.ascontiguousarray(wqkvo),
        "w_up_t": rows_to_partitions(np.asarray(L0_ffn_W_up).T),
        "w_gate_t": rows_to_partitions(np.asarray(L0_ffn_W_gate).T),
        "w_down_t": rows_to_partitions(np.asarray(L0_ffn_W_down).T),
        "ident": np.eye(P, dtype=np.float32),
        "mask": np.concatenate([future, future], axis=1),
        "rope_cos": table(c, c),
        "rope_sin": table(s, -s),
    }
    nc = bacc.Bacc("TRN2", target_bir_lowering=False, num_devices=1)
    args = [nc.dram_tensor(n, a.shape, mybir.dt.from_np(a.dtype), kind="ExternalInput").ap() for n, a in arrays.items()]
    out = nc.dram_tensor("out", (NBATCH, SEQ, E), F32, kind="ExternalOutput").ap()
    macaron_kernel(nc, *args, out)
    return run_bass_kernel_spmd(nc, [arrays], core_ids=[0]).results[0]["out"]
```

```python
from contextlib import ExitStack

import numpy as np

import concourse.bass as bass
from concourse import mybir

ALU = mybir.AluOpType
ACT = mybir.ActivationFunctionType
AX = mybir.AxisListType
F32 = mybir.dt.float32
F16 = mybir.dt.float16
BF16 = mybir.dt.bfloat16
I32 = mybir.dt.int32
RMAX = bass.bass_isa.ReduceOp.max
RADD = bass.bass_isa.ReduceOp.add

P = 128
NBATCH = 16
SEQ = 256
E = 256
HID = 1024
HEADS = 16
HD = E // HEADS
NT = SEQ // P
NC = E // P
W = NT * E
CHUNKS = HID // P
ROUNDS = CHUNKS // 2
SLOTS = HEADS // 2
STK = 4 * HD
VW = 2 * HD + 1

X_SCALE = 2.0 ** 11
W_SCALE = 2.0 ** 14
Q_SCALE = 2.0 ** 6
QKV_OUT = Q_SCALE / (X_SCALE * W_SCALE)
LN_EPS = 1e-5
QUANT_EPS = 1e-8
MASKED = -1.5 * 2.0 ** 127

MISC = [
    ("norm2", 0, "a", 1), ("qk0", 0, "b", 1), ("qk1", 1, "a", 1), ("attn_t", 1, "b", 3), ("out_proj", 2, "a", 3),
    ("v", 2, "b", 1), ("norm3", 3, "b", 3), ("stack_q0", 5, "a", 1), ("stack_k0", 5, "b", 1),
    ("stack_q1", 6, "a", 1), ("stack_k1", 6, "b", 1), ("norm1", 7, "a", -1),
]

PE_SLOT = ["scores", "product_v", "misc_a", "transpose_0", "up_gate", "transpose_1", "misc_b", "down"]
ACT_SLOT = ["misc_a", "prob_hi_0", "tanh", "exps", "prob_hi_1", "misc_b", "hidden_hi"]
ACT_EXTRA = {(3, "hidden_hi"): "rope_hi_0", (4, "hidden_hi"): "rope_hi_1"}
DVE_SLOT = ["row_max", "pv_inverse", "exp_biases", "pv_add", "misc_a", "pv_scale", "prob_lo_0", "silu", "hidden",
            "prob_lo_1", "misc_b"]
DVE_EXTRA = {
    (1, "exp_biases"): ["ffn_added"], (5, "exp_biases"): ["ffn_added"],
    (2, "hidden"): ["rows_3"], (2, "prob_lo_1"): ["stats_3"], (3, "row_max"): ["stats_wait_3"],
    (3, "pv_inverse"): ["mean_3"], (3, "exp_biases"): ["var_3"], (3, "silu"): ["apply_3"],
    (5, "pv_add"): ["rows_1"], (5, "misc_a"): ["stats_1"], (5, "pv_scale"): ["stats_wait_1"],
    (5, "prob_lo_0"): ["mean_1"], (5, "silu"): ["var_1"],
    (6, "exp_biases"): ["rows_2"], (6, "pv_add"): ["stats_2"], (6, "misc_a"): ["stats_wait_2"],
    (6, "pv_scale"): ["mean_2"], (6, "silu"): ["var_2"],
}
POOL_SLOT = [["hidden_lo"], ["mul_0", "hidden_lo"], ["add_0", "mul_1", "hidden_lo"], ["pow_3", "add_1", "hidden_lo"],
             ["lo_00", "lo_01", "hidden_lo"], ["lo_10", "lo_11", "pow_1", "hidden_lo"],
             ["apply_1", "pow_2", "hidden_lo"], ["apply_2", "hidden_lo"]]
STACK_DVE = ("stack_q0", "stack_k0", "stack_q1", "stack_k1")
FIRST_STEP = -1
LOOP_FROM, LOOP_TO = 4, 14
LAST_STEP = NBATCH + 3


def live(b):
    return 0 <= b < NBATCH


def misc_before(t, name):
    index = [m[0] for m in MISC].index(name)
    done = sum(live(u - lag) for u in range(FIRST_STEP, t) for _, _, _, lag in MISC)
    return done + sum(live(t - lag) for _, _, _, lag in MISC[:index])


def misc_through(t, name):
    return misc_before(t, name) + 1


def misc_uses(slot, place):
    return [(name, lag) for name, s, p, lag in MISC if (s, p) == (slot, place)]


def rounds_before(t, slot):
    done = sum(ROUNDS * (live(u) + live(u - 3)) for u in range(0, t))
    return done + (min(slot, ROUNDS) * live(t)) + (max(slot - ROUNDS, 0) * live(t - 3))


class Step:

    def __init__(self, first, i=None):
        self.first, self.i = first, i
        self.parity = first % 2

    def live(self, lag):
        return live(self.first - lag)

    def at(self, count, least=1):
        a = count(self.first)
        if self.i is None:
            return max(a, 0)
        slope = count(self.first + 2) - a
        assert count(self.first + 4) - a == 2 * slope and a >= least
        return self.i * slope + a


def run_steps(engine, body, before={}):
    for t in range(FIRST_STEP, LOOP_FROM):
        if t in before:
            before[t]()
        body(Step(t))
    with engine.Fori(0, (LOOP_TO - LOOP_FROM) // 2) as i:
        body(Step(LOOP_FROM, i))
        body(Step(LOOP_FROM + 1, i))
    for t in range(LOOP_TO, LAST_STEP + 1):
        body(Step(t))


def macaron_kernel(nc, x, wqkvo, w_up_t, w_gate_t, w_down_t, ident, mask, rope_cos, rope_sin, out):
    with ExitStack() as ctx:
        def sb(name, shape, dt=F32):
            return ctx.enter_context(nc.sbuf_tensor(name, shape, dt))

        def ps(name, shape, dt=F32):
            return ctx.enter_context(nc.psum_tensor(name, shape, dt))

        def sem(name):
            return ctx.enter_context(nc.semaphore(name))

        ident_f = sb("ident_f", [P, P])
        ident_h = sb("ident_h", [P, P], F16)
        ident_b = sb("ident_b", [P, P], BF16)
        mask_f = sb("mask_f", [P, 2 * P])
        mask_b = sb("mask_b", [P, 2 * P], BF16)
        cos = sb("cos", [P, NT, 2 * E])
        sin = sb("sin", [P, NT, 2 * E])
        raw_up = sb("raw_up", [P, NC * HID])
        raw_gate = sb("raw_gate", [P, NC * HID])
        raw_down = sb("raw_down", [P, CHUNKS * E])
        raw_w = sb("raw_w", [P, NC, 4, E])
        tern_up = sb("tern_up", [P, NC, HID], F16)
        tern_gate = sb("tern_gate", [P, NC, HID], F16)
        tern_down = sb("tern_down", [P, CHUNKS, E], F16)
        below = sb("below", [P, NC * HID], F16)
        w_hi = sb("w_hi", [P, NC, 4, E], F16)
        w_lo = sb("w_lo", [P, NC, 4, E], F16)
        w_absmax = sb("w_absmax", [P, NC * 4])
        w_max = sb("w_max", [P, 4])
        w_max_all = sb("w_max_all", [P, 4])
        w_pow = sb("w_pow", [P, 4])
        w_inv = sb("w_inv", [P, 4])
        w_mul = sb("w_mul", [P, 4])
        abs_sum = sb("abs_sum", [P, 4])
        abs_sum_all = sb("abs_sum_all", [P, 4])
        tern_scale = sb("tern_scale", [P, 4])
        thr_hi = sb("thr_hi", [P, 4])
        thr_lo = sb("thr_lo", [P, 4])
        scale_prod = sb("scale_prod", [P, 4])
        tanh_scale = sb("tanh_scale", [P, 1])
        down_scale = sb("down_scale", [P, 1])
        exp_scale = sb("exp_scale", [P, 1])
        neg_exp_scale = sb("neg_exp_scale", [P, 1])
        proj_scale = sb("proj_scale", [P, 1])
        minus_half = sb("minus_half", [P, NT])

        xs = sb("xs", [P, NBATCH * W])

        stats = {k: sb(f"stats{k}", [P, NT, 6]) for k in (1, 2, 3)}
        mv = {k: sb(f"mv{k}", [P, NT, 2]) for k in (1, 2, 3)}
        var_s = {k: sb(f"var_s{k}", [P, NT]) for k in (1, 2, 3)}
        rstd = {k: sb(f"rstd{k}", [P, NT]) for k in (1, 2, 3)}
        centred = {k: sb(f"centred{k}", [P, NT, E]) for k in (1, 2)}
        xhat = {k: sb(f"xhat{k}", [P, NT, E]) for k in (1, 2, 3)}
        xt_hi = {k: sb(f"xt_hi{k}", [P, NC, SEQ], F16) for k in (1, 2, 3)}
        xt_lo = {k: sb(f"xt_lo{k}", [P, NC, SEQ], F16) for k in (1, 2, 3)}

        tanh_b = sb("tanh_b", [P, 512])
        silu_b = sb("silu_b", [P, 512])
        hid = sb("hid", [P, 2, 512])
        hid_h = sb("hid_h", [P, 2, 2, SEQ], F16)
        hid_l = sb("hid_l", [P, 2, 2, SEQ], F16)

        qk_rows = sb("qk_rows", [P, NT, 2 * E])
        rope_c = sb("rope_c", [P, NT, 2 * E])
        rope_s = sb("rope_s", [P, NT, 2 * E])
        rope_r = sb("rope_r", [P, NT, 2 * E])
        q_row = sb("q_row", [P, NT, HEADS, 4, HD], F16)
        k_row = sb("k_row", [P, NT, HEADS, 4, HD], F16)
        q_stk = sb("q_stk", [P, 2, SLOTS, SEQ], F16)
        k_stk = sb("k_stk", [P, 2, SLOTS, SEQ], F16)
        v_row = sb("v_row", [P, 2, NT * HEADS, VW], F16)

        neg_max = sb("neg_max", [P, 4])
        exp_bias = sb("exp_bias", [P, 4])
        prob = sb("prob", [P, 2, 2, 384])
        prob_h = sb("prob_h", [P, 2, 2, 384], F16)
        prob_l = sb("prob_l", [P, 2, 2, 384], F16)
        inv_sum = sb("inv_sum", [P, NT, 2, 1])
        pv_sum = sb("pv_sum", [P, NT, 2, HD])
        attn = sb("attn", [P, NT, E])
        attn_h = sb("attn_h", [P, NC, SEQ], F16)
        attn_l = sb("attn_l", [P, NC, SEQ], F16)

        up_ps = ps("up_ps", [P, 512])
        gate_ps = ps("gate_ps", [P, 512])
        down_ps = ps("down_ps", [P, 512])
        score_ps = ps("score_ps", [P, 2, 512])
        probt_ps = ps("probt_ps", [P, 512])
        pv_ps = ps("pv_ps", [P, 512])
        misc_ps = ps("misc_ps", [P, 512])
        misc_h16 = misc_ps[:, :].bitcast(F16)

        x_loaded = [sem("x_even_loaded"), sem("x_odd_loaded")]
        up_loaded, gate_loaded, down_loaded = sem("up_loaded"), sem("gate_loaded"), sem("down_loaded")
        w_loaded, ident_loaded, mask_loaded = sem("w_loaded"), sem("ident_loaded"), sem("mask_loaded")
        rope_loaded, out_stored = sem("rope_loaded"), sem("out_stored")
        abs_done, abs_all, tern_done = sem("abs_done"), sem("abs_all"), sem("tern_done")
        wmax_done, wmax_all, split_done = sem("wmax_done"), sem("wmax_all"), sem("split_done")
        casts_done, ones_done = sem("casts_done"), sem("ones_done")
        scales_done, w_scales_done = sem("scales_done"), sem("w_scales_done")
        misc_written, scores_done, probt_done = sem("misc_written"), sem("scores_done"), sem("probt_done")
        pv_done, up_done, gate_done = sem("pv_done"), sem("up_done"), sem("gate_done")
        down_done = sem("down_done")
        misc_taken = sem("misc_taken")
        stats_done = {k: sem(f"stats_done{k}") for k in (1, 2, 3)}
        mean_done = {k: sem(f"mean_done{k}") for k in (1, 2, 3)}
        var_done = {k: sem(f"var_done{k}") for k in (1, 2, 3)}
        rstd_done = {k: sem(f"rstd_done{k}") for k in (1, 2, 3)}
        centred_done = {k: sem(f"centred_done{k}") for k in (1, 2)}
        xhat_done = {k: sem(f"xhat_done{k}") for k in (1, 2, 3)}
        xt_hi_done = {k: sem(f"xt_hi_done{k}") for k in (1, 2, 3)}
        tanh_done, silu_done, hid_done = sem("tanh_done"), sem("silu_done"), sem("hid_done")
        hid_h_done, hid_l_done = sem("hid_h_done"), sem("hid_l_done")
        rope_mul_done = sem("rope_mul_done")
        rope_done, row_hi_done, row_lo_done = sem("rope_done"), sem("row_hi_done"), sem("row_lo_done")
        v_hi_done = sem("v_hi_done")
        max_done, bias_done, exp_done = sem("max_done"), sem("bias_done"), sem("exp_done")
        prob_h_done, prob_l_done = sem("prob_h_done"), sem("prob_l_done")
        inv_done, pv_sum_done, attn_done = sem("inv_done"), sem("pv_sum_done"), sem("attn_done")
        attn_h_done = sem("attn_h_done")
        ffn1_added, ffn2_added = sem("ffn1_added"), sem("ffn2_added")

        def x_rows(st, lag, lo=0, n=W):
            return xs[:, bass.ds(st.at(lambda t: (t - lag) * W + lo, least=0), n)]

        def copy_stack(engine, st, name, lag, copy):
            tile = int(name[-1])
            stk = q_stk if name.startswith("stack_q") else k_stk
            engine.wait_ge(misc_written, st.at(lambda t: misc_through(t, name)))
            copy(stk[:, (st.first - lag) % 2, :, tile * P:(tile + 1) * P],
                 misc_h16[:, :].rearrange("p (s n) -> p s n", n=P)).then_inc(misc_taken, 1)

        x_dram = x.rearrange("b (n p) e -> b p n e", p=P)
        out_dram = out.rearrange("b (n p) e -> b p n e", p=P)

        block = ctx.enter_context(nc.Block())

        @block.sync
        def _(sp):
            def rows(b):
                return xs[:, bass.ds(b * W, W)].rearrange("p (n e) -> p n e", n=NT)

            sp.dma_start(rows(0), x_dram[0]).then_inc(x_loaded[0], 16)
            sp.dma_start(raw_up[:, :], w_up_t).then_inc(up_loaded, 16)
            sp.dma_start(raw_down[:, :], w_down_t).then_inc(down_loaded, 16)
            sp.dma_start(rows(1), x_dram[1]).then_inc(x_loaded[1], 16)
            sp.dma_start(cos[:, :, :], rope_cos).then_inc(rope_loaded, 16)
            sp.dma_start(sin[:, :, :], rope_sin).then_inc(rope_loaded, 16)
            with sp.Fori(1, NBATCH // 2) as i:
                for b in range(2):
                    sp.wait_ge(x_loaded[b], i * 16)
                    sp.dma_start(xs[:, bass.ds(i * (2 * W) + b * W, W)].rearrange("p (n e) -> p n e", n=NT),
                                 x_dram[bass.ds(i * 2 + b, 1)].rearrange("o p n e -> (o p) n e")
                                 ).then_inc(x_loaded[b], 16)
            with sp.Fori(0, NBATCH) as b:
                sp.wait_ge(ffn2_added, b + 1)
                sp.dma_start(out_dram[bass.ds(b, 1)].rearrange("o p n e -> (o p) n e"),
                             xs[:, bass.ds(b * W, W)].rearrange("p (n e) -> p n e", n=NT)
                             ).then_inc(out_stored, 16)
            sp.wait_ge(out_stored, 16 * NBATCH)

        @block.tensor
        def _(pe):
            def split_product(dst, pairs, flags):
                for n, (lhs, rhs) in enumerate(pairs):
                    mm = pe.matmul(dst, lhs, rhs, start=flags and n == 0, stop=n == len(pairs) - 1,
                                   skip_group_check=True)
                return mm

            def three(a_hi, a_lo, b_hi, b_lo):
                return [(a_hi, b_hi), (a_hi, b_lo), (a_lo, b_hi)]

            def scores(st, s):
                pe.wait_ge(misc_taken, st.at(lambda t: misc_through(t - 1, "stack_k1")))
                pe.wait_ge(exp_done, st.at(lambda t: SLOTS * (t - 2) + s))
                par = st.parity
                for j in range(2):
                    pe.matmul(score_ps[:, j, P:3 * P], ident_b[:, :], mask_b[:, :], start=True, stop=False,
                              skip_group_check=True)
                for j in range(2):
                    q = q_stk[STK * j:STK * (j + 1), par, s, :]
                    k = k_stk[STK * j:STK * (j + 1), par, s, :]
                    pe.matmul(score_ps[:, j, 0:2 * P], q[:, P:2 * P], k[:, 0:2 * P], start=False, stop=True,
                              skip_group_check=True)
                    mm = pe.matmul(score_ps[:, j, 2 * P:3 * P], q[:, 0:P], k[:, 0:P], start=False, stop=True,
                                   skip_group_check=True)
                mm.then_inc(scores_done, 1)

            def pair_of(s, back):
                return (2, s - back) if s >= back else (3, s - back + SLOTS)

            def product_v(st, s):
                lag, pair = pair_of(s, 2)
                if not st.live(lag):
                    return
                pe.wait_ge(prob_l_done, st.at(lambda t: 2 * (SLOTS * (t - lag) + pair + 1)))
                pe.wait_ge(pv_sum_done, st.at(lambda t: SLOTS * (t - lag) + pair))
                v = v_row[:, (st.first - lag) % 2, :, :].rearrange("p (n h) w -> p n h w", n=NT)
                first = True
                for j in range(2):
                    h = 2 * pair + j
                    for tile, blocks in ((0, [(0, 0)]), (1, [(1, 0), (2, 1)])):
                        dst = pv_ps[:, (2 * tile + j) * VW:(2 * tile + j + 1) * VW]
                        for col, keys in blocks:
                            for part in (prob_h, prob_l):
                                mm = pe.matmul(dst, part[:, pair % 2, j, col * P:(col + 1) * P], v[:, keys, h, :],
                                               start=first, stop=True, skip_group_check=True)
                                first = False
                mm.then_inc(pv_done, 1)

            def transpose_probs(st, s, j):
                lag, pair = pair_of(s, 1)
                if not st.live(lag):
                    return
                if j == 0:
                    pe.wait_ge(exp_done, st.at(lambda t: SLOTS * (t - lag) + pair + 1))
                pe.wait_ge(prob_l_done, st.at(lambda t: 2 * (SLOTS * (t - lag) + pair) + j))
                for n, col in enumerate((2, 0, 1)):
                    mm = pe.transpose(probt_ps[:, n * P:(n + 1) * P], prob[:, pair % 2, j, col * P:(col + 1) * P],
                                      ident_f[:, :])
                mm.then_inc(probt_done, 1)

            def up_gate(st, s):
                k, lag, r = (1, 0, s) if s < ROUNDS else (3, 3, s - ROUNDS)
                if not st.live(lag):
                    return
                pe.wait_ge(misc_taken, st.at(
                    lambda t: misc_through(t - 1, "norm1") if k == 1 else misc_through(t, "norm3")))
                pe.wait_ge(silu_done, st.at(lambda t: rounds_before(t, s)))
                for dst, tern, done in ((up_ps, tern_up, up_done), (gate_ps, tern_gate, gate_done)):
                    if dst is gate_ps:
                        pe.wait_ge(hid_done, st.at(lambda t: rounds_before(t, s)))
                    for m in range(2):
                        at = (2 * r + m) * P
                        pairs = [(tern[:, c, at:at + P], part[:, c, :]) for c in range(NC)
                                 for part in (xt_hi[k], xt_lo[k])]
                        mm = split_product(dst[:, m * SEQ:(m + 1) * SEQ], pairs, m == 0)
                    mm.then_inc(done, 1)

            def down(st, s):
                lag, r = [(4, 3), (0, 0), (0, 1), (0, 2), (0, 3), (3, 0), (3, 1), (3, 2)][s]
                if not st.live(lag):
                    return
                pe.wait_ge(hid_l_done, st.at(lambda t: rounds_before(t, s)))
                if r == 0:
                    if lag == 0:
                        pe.wait_ge(ffn2_added, st.at(lambda t: t - 3))
                    else:
                        pe.wait_ge(ffn1_added, st.at(lambda t: min(t + 1, NBATCH)))
                par = r % 2
                for tile in range(NT):
                    pairs = [(part[:, par, m, tile * P:(tile + 1) * P], tern_down[:, 2 * r + m, :])
                             for m in range(2) for part in (hid_h, hid_l)]
                    mm = split_product(down_ps[:, tile * E:(tile + 1) * E], pairs, r == 0 and tile == 0)
                mm.then_inc(down_done, 1)

            def transpose_rows(src):
                for c in range(NC):
                    for tile in range(NT):
                        mm = pe.transpose(misc_ps[:, c * SEQ + tile * P:c * SEQ + (tile + 1) * P],
                                          src[:, tile, c * P:(c + 1) * P], ident_f[:, :])
                return mm

            def misc(st, s, place):
                for name, lag in misc_uses(s, place):
                    if not st.live(lag):
                        continue
                    pe.wait_ge(misc_taken, st.at(lambda t: misc_before(t, name)))
                    if name.startswith("norm"):
                        k = int(name[-1])
                        pe.wait_ge(xhat_done[k], st.at(lambda t: t - lag + 1))
                        mm = transpose_rows(xhat[k])
                    elif name in ("qk0", "qk1"):
                        tile = int(name[-1])
                        pe.wait_ge(split_done, 8)
                        rows = slice(tile * P, (tile + 1) * P)
                        pairs = [p for c in range(NC) for p in three(
                            xt_hi[2][:, c, rows], xt_lo[2][:, c, rows],
                            w_hi[:, c, 0:2, :].rearrange("p m e -> p (m e)"),
                            w_lo[:, c, 0:2, :].rearrange("p m e -> p (m e)"))]
                        mm = split_product(misc_ps[:, :], pairs, True)
                    elif name == "v":
                        for tile in range(NT):
                            rows = slice(tile * P, (tile + 1) * P)
                            pairs = [p for c in range(NC) for p in three(
                                xt_hi[2][:, c, rows], xt_lo[2][:, c, rows], w_hi[:, c, 2, :], w_lo[:, c, 2, :])]
                            mm = split_product(misc_ps[:, tile * E:(tile + 1) * E], pairs, tile == 0)
                    elif name == "attn_t":
                        pe.wait_ge(attn_done, st.at(lambda t: SLOTS * (t - lag + 1)))
                        mm = transpose_rows(attn)
                    elif name == "out_proj":
                        for tile in range(NT):
                            rows = slice(tile * P, (tile + 1) * P)
                            pairs = [p for c in range(NC) for p in three(
                                attn_h[:, c, rows], attn_l[:, c, rows], w_hi[:, c, 3, :], w_lo[:, c, 3, :])]
                            mm = split_product(misc_ps[:, tile * E:(tile + 1) * E], pairs, tile == 0)
                    else:
                        tile = int(name[-1])
                        row = q_row if name.startswith("stack_q") else k_row
                        pe.wait_ge(row_lo_done, st.at(lambda t: 4 * (t - lag) + 2 * tile + (2 if row is k_row else 1)))
                        for pair in range(SLOTS):
                            mm = pe.transpose(misc_h16[:, pair * P:(pair + 1) * P],
                                              row[:, tile, 2 * pair:2 * pair + 2, :, :].rearrange("p h s d -> p (h s d)"),
                                              ident_h[:, :])
                    mm.then_inc(misc_written, 1)

            def step(st):
                for s in range(SLOTS):
                    for what in PE_SLOT:
                        if what == "scores" and st.live(2):
                            scores(st, s)
                        elif what == "product_v":
                            product_v(st, s)
                        elif what.startswith("misc"):
                            misc(st, s, what[-1])
                        elif what.startswith("transpose"):
                            transpose_probs(st, s, int(what[-1]))
                        elif what == "up_gate":
                            up_gate(st, s)
                        elif what == "down":
                            down(st, s)

            pe.wait_ge(casts_done, 4)
            pe.wait_ge(ident_loaded, 16)
            run_steps(pe, step, before={0: lambda: pe.wait_ge(tern_done, 3)})

        @block.scalar
        def _(act):
            def set_up_loads():
                act.dma_start(raw_gate[:, :], w_gate_t).then_inc(gate_loaded, 16)
                act.dma_start(ident_f[:, :], ident).then_inc(ident_loaded, 16)
                act.dma_start(mask_f[:, :], mask).then_inc(mask_loaded, 16)
                act.dma_start(raw_w[:, :, :, :], wqkvo).then_inc(w_loaded, 16)

            def set_up():
                for n, (raw, junk, loaded) in enumerate((
                        (raw_up, tern_up, up_loaded), (raw_gate, tern_gate, gate_loaded),
                        (raw_down, tern_down, down_loaded))):
                    act.wait_ge(loaded, 16)
                    act.activation(junk[:, :, :].rearrange("p a b -> p (a b)"), raw[:, :], ACT.Abs,
                                   accum_out=abs_sum[:, n:n + 1]).then_inc(abs_done, 1)
                act.wait_ge(scales_done, 6)

            def split_misc(st, name, lag, dst, done):
                act.wait_ge(misc_written, st.at(lambda t: misc_through(t, name)))
                act.activation(dst[:, :, :].rearrange("p c n -> p (c n)"), misc_ps[:, :], ACT.Copy).then_inc(done, 1)

            def misc(st, s, place):
                for name, lag in misc_uses(s, place):
                    if not st.live(lag):
                        continue
                    if name.startswith("norm"):
                        k = int(name[-1])
                        split_misc(st, name, lag, xt_hi[k], xt_hi_done[k])
                    elif name == "attn_t":
                        split_misc(st, name, lag, attn_h, attn_h_done)
                    elif name in ("qk0", "qk1"):
                        act.wait_ge(misc_written, st.at(lambda t: misc_through(t, name)))
                        act.activation(qk_rows[:, int(name[-1]), :], misc_ps[:, :], ACT.Copy).then_inc(misc_taken, 1)
                    elif name == "v":
                        act.wait_ge(ones_done, 1)
                        act.wait_ge(misc_written, st.at(lambda t: misc_through(t, name)))
                        act.activation(v_row[:, (st.first - lag) % 2, :, 0:HD],
                                       misc_ps[:, :].rearrange("p (m d) -> p m d", d=HD), ACT.Copy,
                                       scale=QKV_OUT).then_inc(v_hi_done, 1)
                    elif name.startswith("stack") and name not in STACK_DVE:
                        copy_stack(act, st, name, lag, lambda dst, src: act.activation(dst, src, ACT.Copy))

            def rope_hi(st, tile):
                if not st.live(1):
                    return
                act.wait_ge(rope_done, st.at(lambda t: 2 * (t - 1) + tile + 1))
                r = rope_r[:, tile, :].rearrange("p (m h d) -> p m h d", m=2, d=HD)
                for m, (row, places) in enumerate(((q_row, slice(0, 4, 3)), (k_row, slice(0, 4, 2)))):
                    dst = row[:, tile, :, places, :]
                    src = r[:, m, :, None, :].to_broadcast([P, HEADS, 2, HD])
                    act.activation(dst, src, ACT.Copy).then_inc(row_hi_done, 1)

            def prob_hi(st, s, j):
                lag, pair = (2, s - 1) if s else (3, SLOTS - 1)
                if not st.live(lag):
                    return
                act.wait_ge(probt_done, st.at(lambda t: 2 * (SLOTS * (t - lag) + pair) + j + 1))
                act.activation(prob_h[:, pair % 2, j, :], probt_ps[:, 0:384], ACT.Copy).then_inc(prob_h_done, 1)

            def exps(st, s):
                act.wait_ge(bias_done, st.at(lambda t: SLOTS * (t - 2) + s + 1))
                for j in range(2):
                    act.activation(prob[:, s % 2, j, 0:256], score_ps[:, j, 0:256], ACT.Exp,
                                   bias=exp_bias[:, j:j + 1], scale=exp_scale[:, :])
                    a = act.activation(prob[:, s % 2, j, 256:384], score_ps[:, j, 256:384], ACT.Exp,
                                       bias=exp_bias[:, 2 + j:3 + j], scale=exp_scale[:, :])
                a.then_inc(exp_done, 1)

            def tanh(st, s):
                if not st.live(0 if s < ROUNDS else 3):
                    return
                act.wait_ge(up_done, st.at(lambda t: rounds_before(t, s) + 1))
                act.activation(tanh_b[:, :], up_ps[:, :], ACT.Tanh, scale=tanh_scale[:, :]).then_inc(tanh_done, 1)

            def hidden_hi(st, s):
                if not st.live(0 if s < ROUNDS else 3):
                    return
                act.wait_ge(hid_done, st.at(lambda t: rounds_before(t, s) + 1))
                act.activation(hid_h[:, s % 2, :, :].rearrange("p m n -> p (m n)"), hid[:, s % 2, :],
                               ACT.Copy).then_inc(hid_h_done, 1)

            def step(st):
                for s in range(SLOTS):
                    for what in ACT_SLOT:
                        if (s, what) in ACT_EXTRA:
                            rope_hi(st, int(ACT_EXTRA[s, what][-1]))
                        if what.startswith("misc"):
                            misc(st, s, what[-1])
                        elif what.startswith("prob_hi"):
                            prob_hi(st, s, int(what[-1]))
                        elif what == "exps" and st.live(2):
                            exps(st, s)
                        elif what == "tanh":
                            tanh(st, s)
                        elif what == "hidden_hi":
                            hidden_hi(st, s)

            set_up_loads()
            run_steps(act, step, before={0: set_up})

        @block.vector
        def _(dve):
            def set_up_constants():
                dve.memset(minus_half[:, :], -0.5).then_inc(casts_done, 1)
                dve.memset(v_row[:, :, :, 2 * HD:VW], 1.0).then_inc(ones_done, 1)
                dve.wait_ge(ident_loaded, 16)
                dve.tensor_copy(ident_h[:, :], ident_f[:, :]).then_inc(casts_done, 1)
                dve.wait_ge(mask_loaded, 16)
                dve.tensor_copy(mask_b[:, :], mask_f[:, :]).then_inc(casts_done, 1)
                dve.tensor_copy(ident_b[:, :], ident_f[:, :]).then_inc(casts_done, 1)

            def set_up_ternary():
                dve.wait_ge(abs_all, 1)
                dve.tensor_scalar(tern_scale[:, 0:3], abs_sum_all[:, 0:3], 1.0 / (E * HID), QUANT_EPS,
                                  ALU.mult, ALU.add).then_inc(scales_done, 1)
                dve.wait_ge(scales_done, 1)
                dve.tensor_scalar(thr_hi[:, 0:3], tern_scale[:, 0:3], 0.5, None, ALU.mult).then_inc(scales_done, 1)
                dve.tensor_scalar(thr_lo[:, 0:3], tern_scale[:, 0:3], -0.5, None, ALU.mult).then_inc(scales_done, 1)
                dve.tensor_tensor(scale_prod[:, 0:1], tern_scale[:, 0:1], tern_scale[:, 1:2], ALU.mult
                                  ).then_inc(scales_done, 1)
                dve.wait_ge(scales_done, 4)
                dve.tensor_scalar(tanh_scale[:, :], tern_scale[:, 0:1], 0.5 / X_SCALE, None, ALU.mult
                                  ).then_inc(scales_done, 1)
                dve.tensor_tensor(down_scale[:, :], scale_prod[:, 0:1], tern_scale[:, 2:3], ALU.mult
                                  ).then_inc(scales_done, 1)
                for n, (raw, tern) in enumerate(((raw_up, tern_up), (raw_gate, tern_gate), (raw_down, tern_down))):
                    if n:
                        dve.wait_ge(tern_done, n)
                    dve.tensor_scalar(below[:, :], raw[:, :], thr_lo[:, n:n + 1], None, ALU.is_lt
                                      ).then_inc(scales_done, 1)
                    dve.wait_ge(scales_done, 7 + n)
                    dve.scalar_tensor_tensor(out=tern[:, :, :].rearrange("p a b -> p (a b)"), in0=raw[:, :],
                                             scalar=thr_hi[:, n:n + 1], in1=below[:, :], op0=ALU.is_gt,
                                             op1=ALU.subtract).then_inc(tern_done, 1)

            def split_weights():
                dve.wait_ge(w_loaded, 16)
                dve.tensor_reduce(w_absmax[:, :], raw_w[:, :, :, :].rearrange("p c m e -> p (c m) e"), AX.X, ALU.max,
                                  apply_absolute_value=True).then_inc(w_scales_done, 1)
                dve.wait_ge(w_scales_done, 1)
                dve.tensor_tensor(w_max[:, :], w_absmax[:, 0:4], w_absmax[:, 4:8], ALU.max).then_inc(wmax_done, 1)
                dve.wait_ge(wmax_all, 1)
                dve.tensor_scalar(w_max[:, :], w_max_all[:, :], 1e-30, None, ALU.max).then_inc(w_scales_done, 1)
                dve.wait_ge(w_scales_done, 2)
                dve.tensor_scalar(w_pow[:, :].bitcast(I32), w_max[:, :].bitcast(I32), 0x7F800000, None,
                                  ALU.bitwise_and).then_inc(w_scales_done, 1)
                dve.wait_ge(w_scales_done, 3)
                dve.reciprocal(w_inv[:, :], w_pow[:, :]).then_inc(w_scales_done, 1)
                dve.tensor_tensor(scale_prod[:, 1:2], w_pow[:, 0:1], w_pow[:, 1:2], ALU.mult).then_inc(w_scales_done, 1)
                dve.tensor_tensor(scale_prod[:, 2:3], w_pow[:, 2:3], w_pow[:, 3:4], ALU.mult).then_inc(w_scales_done, 1)
                dve.wait_ge(w_scales_done, 6)
                dve.tensor_scalar(w_mul[:, :], w_inv[:, :], W_SCALE, None, ALU.mult).then_inc(w_scales_done, 1)
                to_scores = 1.0 / (Q_SCALE * Q_SCALE * HD ** 0.5)
                dve.tensor_scalar(neg_exp_scale[:, :], scale_prod[:, 1:2], -to_scores, None, ALU.mult
                                  ).then_inc(w_scales_done, 1)
                dve.tensor_scalar(proj_scale[:, :], scale_prod[:, 2:3], 1.0 / (Q_SCALE * W_SCALE), None, ALU.mult
                                  ).then_inc(w_scales_done, 1)
                dve.tensor_scalar(exp_scale[:, :], scale_prod[:, 1:2], to_scores, None, ALU.mult).then_inc(w_scales_done, 1)
                dve.wait_ge(w_scales_done, 10)
                for m in range(4):
                    dve.tensor_scalar(w_hi[:, :, m, :], raw_w[:, :, m, :], w_mul[:, m:m + 1], None, ALU.mult
                                      ).then_inc(split_done, 1)
                for m in range(4):
                    dve.wait_ge(split_done, m + 1)
                    dve.scalar_tensor_tensor(out=w_lo[:, :, m, :], in0=raw_w[:, :, m, :], scalar=w_mul[:, m:m + 1],
                                             in1=w_hi[:, :, m, :], op0=ALU.mult, op1=ALU.subtract
                                             ).then_inc(split_done, 1)
                dve.wait_ge(rope_loaded, 32)

            def wait_norm_rows(st, k, lag):
                if not st.live(lag):
                    return
                if k == 1:
                    dve.wait_ge(x_loaded[(st.first - lag) % 2], st.at(lambda t: 16 * ((t - lag) // 2) + 16))
                elif k == 2:
                    dve.wait_ge(ffn1_added, st.at(lambda t: t - lag + 1))
                else:
                    dve.wait_ge(misc_taken, st.at(lambda t: misc_through(t, "out_proj")))

            def norm_stats(st, k, lag):
                if st.live(lag):
                    for tile in range(NT):
                        dve.bn_stats(stats[k][:, tile, :], x_rows(st, lag, tile * E, E)).then_inc(stats_done[k], 1)

            def wait_stats(st, k, lag):
                if st.live(lag):
                    dve.wait_ge(stats_done[k], st.at(lambda t: 2 * (t - lag + 1)))

            def norm_mean(st, k, lag):
                if st.live(lag):
                    for tile in range(NT):
                        dve.bn_aggr(mv[k][:, tile, :], stats[k][:, tile, :]).then_inc(mean_done[k], 1)

            def norm_var(st, k, lag):
                if st.live(lag):
                    dve.wait_ge(mean_done[k], st.at(lambda t: 2 * (t - lag + 1)))
                    dve.tensor_scalar(var_s[k][:, :, None], mv[k][:, :, 1:2], X_SCALE ** -2, LN_EPS * X_SCALE ** -2,
                                      ALU.mult, ALU.add).then_inc(var_done[k], 1)

            def norm_apply(st, k, lag):
                if not st.live(lag):
                    return
                dve.wait_ge(rstd_done[k], st.at(lambda t: t - lag + 1))
                for tile in range(NT):
                    a = dve.tensor_scalar(xhat[k][:, tile, :], x_rows(st, lag, tile * E, E), mv[k][:, tile, 0:1],
                                          rstd[k][:, tile:tile + 1], ALU.subtract, ALU.mult)
                a.then_inc(xhat_done[k], 1)

            def add_residual(st, src, scale, lag, done):
                rows = x_rows(st, lag)
                return dve.scalar_tensor_tensor(out=rows, in0=src[:, :], scalar=scale[:, :], in1=x_rows(st, lag),
                                                op0=ALU.mult, op1=ALU.add).then_inc(done, 1)

            def ffn_added(st, s):
                lag, done = {1: (4, ffn2_added), 5: (0, ffn1_added)}[s]
                if not st.live(lag):
                    return
                dve.wait_ge(down_done, st.at(lambda t: rounds_before(t, s - 1)))
                add_residual(st, down_ps, down_scale, lag, done)

            def low_part(st, lag, dst, high, hi_done):
                dve.wait_ge(hi_done, st.at(lambda t: t - lag + 1))
                dve.tensor_tensor(dst[:, :, :].rearrange("p c n -> p (c n)"), misc_ps[:, :],
                                  high[:, :, :].rearrange("p c n -> p (c n)"), ALU.subtract).then_inc(misc_taken, 1)

            def misc(st, s, place):
                for name, lag in misc_uses(s, place):
                    if not st.live(lag):
                        continue
                    if name.startswith("norm"):
                        k = int(name[-1])
                        low_part(st, lag, xt_lo[k], xt_hi[k], xt_hi_done[k])
                    elif name == "attn_t":
                        low_part(st, lag, attn_l, attn_h, attn_h_done)
                    elif name in STACK_DVE:
                        copy_stack(dve, st, name, lag, dve.tensor_copy)
                    elif name == "v":
                        v = v_row[:, (st.first - lag) % 2, :, :]
                        dve.wait_ge(v_hi_done, st.at(lambda t: t - lag + 1))
                        dve.scalar_tensor_tensor(out=v[:, :, HD:2 * HD],
                                                 in0=misc_ps[:, :].rearrange("p (m d) -> p m d", d=HD),
                                                 scalar=QKV_OUT, in1=v[:, :, 0:HD], op0=ALU.mult,
                                                 op1=ALU.subtract).then_inc(misc_taken, 1)
                    elif name == "out_proj":
                        dve.wait_ge(misc_written, st.at(lambda t: misc_through(t, name)))
                        add_residual(st, misc_ps, proj_scale, lag, misc_taken)

            def row_max(st, s):
                dve.wait_ge(scores_done, st.at(lambda t: SLOTS * (t - 2) + s + 1))
                dve.tensor_reduce(neg_max[:, 0:2], score_ps[:, :, 0:256], AX.X, ALU.max, negate=True)
                dve.tensor_reduce(neg_max[:, 2:4], score_ps[:, :, 256:384], AX.X, ALU.max, negate=True
                                  ).then_inc(max_done, 1)

            def exp_biases(st, s):
                dve.wait_ge(max_done, st.at(lambda t: SLOTS * (t - 2) + s + 1))
                dve.tensor_scalar(exp_bias[:, :], neg_max[:, :], exp_scale[:, :], None, ALU.mult
                                  ).then_inc(bias_done, 1)

            def pv_parts(s):
                return (2, s - 2) if s >= 2 else (3, s - 2 + SLOTS)

            pv = pv_ps[:, 0:4 * VW].rearrange("p (n j w) -> p n j w", n=NT, j=2)

            def pv_inverse(st, s):
                lag, pair = pv_parts(s)
                if st.live(lag):
                    dve.wait_ge(pv_done, st.at(lambda t: SLOTS * (t - lag) + pair + 1))
                    dve.reciprocal(inv_sum[:, :, :, :], pv[:, :, :, 2 * HD:VW]).then_inc(inv_done, 1)

            def pv_add(st, s):
                lag, pair = pv_parts(s)
                if st.live(lag):
                    dve.wait_ge(pv_done, st.at(lambda t: SLOTS * (t - lag) + pair + 1))
                    dve.tensor_reduce(pv_sum[:, :, :, :].rearrange("p n j d -> p (n j) d"),
                                      pv_ps[:, 0:4 * VW].rearrange("p (m w) -> p m w", w=VW)[:, :, 0:2 * HD]
                                      .rearrange("p m (a d) -> p m d a", a=2), AX.X, ALU.add
                                      ).then_inc(pv_sum_done, 1)

            def pv_scale(st, s):
                lag, pair = pv_parts(s)
                if st.live(lag):
                    if pair == 0:
                        dve.wait_ge(attn_h_done, st.at(lambda t: t - lag))
                    dve.wait_ge(inv_done, st.at(lambda t: SLOTS * (t - lag) + pair + 1))
                    dve.wait_ge(pv_sum_done, st.at(lambda t: SLOTS * (t - lag) + pair + 1))
                    dve.tensor_tensor(attn[:, :, 2 * pair * HD:2 * (pair + 1) * HD]
                                      .rearrange("p n (j d) -> p n j d", j=2), pv_sum[:, :, :, :],
                                      inv_sum[:, :, :, :].to_broadcast([P, NT, 2, HD]), ALU.mult
                                      ).then_inc(attn_done, 1)

            def prob_lo(st, s, j):
                lag, pair = (2, s - 1) if s else (3, SLOTS - 1)
                if not st.live(lag):
                    return
                dve.wait_ge(prob_h_done, st.at(lambda t: 2 * (SLOTS * (t - lag) + pair) + j + 1))
                dve.tensor_tensor(prob_l[:, pair % 2, j, :], probt_ps[:, 0:384], prob_h[:, pair % 2, j, :],
                                  ALU.subtract).then_inc(prob_l_done, 1)

            def silu(st, s):
                if not st.live(0 if s < ROUNDS else 3):
                    return
                dve.wait_ge(tanh_done, st.at(lambda t: rounds_before(t, s) + 1))
                dve.scalar_tensor_tensor(out=silu_b[:, :], in0=tanh_b[:, :], scalar=1.0, in1=up_ps[:, :],
                                         op0=ALU.add, op1=ALU.mult).then_inc(silu_done, 1)

            def hidden(st, s):
                if not st.live(0 if s < ROUNDS else 3):
                    return
                dve.wait_ge(hid_l_done, st.at(lambda t: rounds_before(t, s) - 1))
                dve.wait_ge(gate_done, st.at(lambda t: rounds_before(t, s) + 1))
                dve.wait_ge(silu_done, st.at(lambda t: rounds_before(t, s) + 1))
                dve.scalar_tensor_tensor(out=hid[:, s % 2, :], in0=silu_b[:, :], scalar=0.25 / X_SCALE ** 2,
                                         in1=gate_ps[:, :], op0=ALU.mult, op1=ALU.mult).then_inc(hid_done, 1)

            lag_of_norm = {1: -1, 2: 0, 3: 3}
            norm_parts = {"rows": wait_norm_rows, "stats": norm_stats, "stats_wait": wait_stats, "mean": norm_mean,
                          "var": norm_var, "apply": norm_apply}
            parts = {"pv_inverse": pv_inverse, "pv_add": pv_add, "pv_scale": pv_scale, "silu": silu, "hidden": hidden}

            def step(st):
                for s in range(SLOTS):
                    for what in DVE_SLOT:
                        for extra in DVE_EXTRA.get((s, what), []):
                            if extra == "ffn_added":
                                ffn_added(st, s)
                            else:
                                k = int(extra[-1])
                                norm_parts[extra[:-2]](st, k, lag_of_norm[k])
                        if what in parts:
                            parts[what](st, s)
                        elif what.startswith("misc"):
                            misc(st, s, what[-1])
                        elif what.startswith("prob_lo"):
                            prob_lo(st, s, int(what[-1]))
                        elif what == "row_max" and st.live(2):
                            row_max(st, s)
                        elif what == "exp_biases" and st.live(2):
                            exp_biases(st, s)

            set_up_constants()
            run_steps(dve, step, before={0: set_up_ternary, 1: split_weights})

        @block.gpsimd
        def _(pool):
            def rstd_power(st, k, lag):
                if not st.live(lag):
                    return
                pool.wait_ge(var_done[k], st.at(lambda t: t - lag + 1))
                pool.tensor_tensor(rstd[k][:, :], var_s[k][:, :], minus_half[:, :], ALU.pow).then_inc(rstd_done[k], 1)

            def norm_apply(st, k, lag):
                if not st.live(lag):
                    return
                rows = x_rows(st, lag).rearrange("p (n e) -> p n e", n=NT)
                pool.tensor_tensor(centred[k][:, :, :], rows, mv[k][:, :, 0:1].to_broadcast([P, NT, E]), ALU.subtract
                                   ).then_inc(centred_done[k], 1)
                pool.wait_ge(centred_done[k], st.at(lambda t: t - lag + 1))
                pool.wait_ge(rstd_done[k], st.at(lambda t: t - lag + 1))
                pool.tensor_tensor(xhat[k][:, :, :], centred[k][:, :, :], rstd[k][:, :, None].to_broadcast([P, NT, E]),
                                   ALU.mult).then_inc(xhat_done[k], 1)

            def rope_mul(st, tile):
                if not st.live(1):
                    return
                pool.wait_ge(misc_taken, st.at(lambda t: misc_through(t, f"qk{tile}")))
                pool.tensor_tensor(rope_c[:, tile, :], qk_rows[:, tile, :], cos[:, tile, :], ALU.mult)
                pool.tensor_tensor(rope_s[:, tile, :], qk_rows[:, tile, :], sin[:, tile, :], ALU.mult
                                   ).then_inc(rope_mul_done, 1)

            def rope_add(st, tile):
                if not st.live(1):
                    return
                pool.wait_ge(rope_mul_done, st.at(lambda t: 2 * (t - 1) + tile + 1))

                def halves(a):
                    return a[:, tile, :].rearrange("p (h a d) -> p h a d", a=2, d=HD // 2)

                pool.tensor_tensor(halves(rope_r), halves(rope_c), halves(rope_s)[:, :, ::-1, :], ALU.add
                                   ).then_inc(rope_done, 1)

            def row_lo(st, tile, m):
                if not st.live(1):
                    return
                row, places = ((q_row, slice(1, 3)), (k_row, slice(1, 4, 2)))[m]
                r = rope_r[:, tile, :].rearrange("p (m h d) -> p m h d", m=2, d=HD)[:, m]
                pool.wait_ge(row_hi_done, st.at(lambda t: 4 * (t - 1) + 2 * tile + m + 1))
                pool.tensor_tensor(row[:, tile, :, places, :], r[:, :, None, :].to_broadcast([P, HEADS, 2, HD]),
                                   row[:, tile, :, 0:1, :].to_broadcast([P, HEADS, 2, HD]), ALU.subtract
                                   ).then_inc(row_lo_done, 1)

            def hidden_lo(st, s):
                if not st.live(0 if s < ROUNDS else 3):
                    return
                pool.wait_ge(hid_h_done, st.at(lambda t: rounds_before(t, s) + 1))
                pool.tensor_tensor(hid_l[:, s % 2, :, :].rearrange("p m n -> p (m n)"), hid[:, s % 2, :],
                                   hid_h[:, s % 2, :, :].rearrange("p m n -> p (m n)"), ALU.subtract
                                   ).then_inc(hid_l_done, 1)

            def step(st):
                lag_of_norm = {1: -1, 2: 0, 3: 3}
                for s in range(SLOTS):
                    for what in POOL_SLOT[s]:
                        if what == "hidden_lo":
                            hidden_lo(st, s)
                        elif what.startswith("mul"):
                            rope_mul(st, int(what[-1]))
                        elif what.startswith("add"):
                            rope_add(st, int(what[-1]))
                        elif what.startswith("lo"):
                            row_lo(st, int(what[-2]), int(what[-1]))
                        elif what.startswith("pow"):
                            rstd_power(st, int(what[-1]), lag_of_norm[int(what[-1])])
                        elif what.startswith("apply"):
                            norm_apply(st, int(what[-1]), lag_of_norm[int(what[-1])])

            def sum_all():
                pool.wait_ge(abs_done, 3)
                pool.partition_all_reduce(abs_sum_all[:, 0:3], abs_sum[:, 0:3], P, RADD).then_inc(abs_all, 1)

            def max_all():
                pool.wait_ge(wmax_done, 1)
                pool.partition_all_reduce(w_max_all[:, :], w_max[:, :], P, RMAX).then_inc(wmax_all, 1)

            pool.wait_ge(casts_done, 1)
            run_steps(pool, step, before={0: sum_all, 1: max_all})


def kernel(L0_attn_x, L0_attn_wq, L0_attn_wk, L0_attn_wv, L0_attn_wo, L0_ffn_W_up, L0_ffn_W_gate, L0_ffn_W_down):
    import concourse.bacc as bacc
    from concourse.bass_utils import run_bass_kernel_spmd

    def rows_to_partitions(a):
        a = np.ascontiguousarray(a)
        return np.ascontiguousarray(a.reshape(a.shape[0] // P, P, a.shape[1]).transpose(1, 0, 2).reshape(P, -1))

    wqkvo = np.stack([rows_to_partitions(w).reshape(P, NC, E)
                      for w in (L0_attn_wq, L0_attn_wk, L0_attn_wv, L0_attn_wo)], axis=2)

    freq = (1.0 / np.float32(10000.0) ** (np.arange(0, HD, 2, dtype=np.float32) / np.float32(HD))).astype(np.float32)
    angle = np.arange(SEQ, dtype=np.float32)[:, None] * freq[None, :]
    s, c = np.sin(angle) * np.float32(QKV_OUT), np.cos(angle) * np.float32(QKV_OUT)

    def table(first_half, second_half):
        head = np.concatenate([first_half, second_half], axis=1).astype(np.float32)
        return np.ascontiguousarray(np.tile(head, (1, 2 * HEADS)).reshape(NT, P, 2 * E).transpose(1, 0, 2))

    future = np.triu(np.full((P, P), MASKED, dtype=np.float32), k=1)
    arrays = {
        "x": np.ascontiguousarray(L0_attn_x),
        "wqkvo": np.ascontiguousarray(wqkvo),
        "w_up_t": rows_to_partitions(np.asarray(L0_ffn_W_up).T),
        "w_gate_t": rows_to_partitions(np.asarray(L0_ffn_W_gate).T),
        "w_down_t": rows_to_partitions(np.asarray(L0_ffn_W_down).T),
        "ident": np.eye(P, dtype=np.float32),
        "mask": np.concatenate([future, future], axis=1),
        "rope_cos": table(c, c),
        "rope_sin": table(s, -s),
    }
    nc = bacc.Bacc("TRN2", target_bir_lowering=False, num_devices=1)
    args = [nc.dram_tensor(n, a.shape, mybir.dt.from_np(a.dtype), kind="ExternalInput").ap() for n, a in arrays.items()]
    out = nc.dram_tensor("out", (NBATCH, SEQ, E), F32, kind="ExternalOutput").ap()
    macaron_kernel(nc, *args, out)
    return run_bass_kernel_spmd(nc, [arrays], core_ids=[0]).results[0]["out"]
```

```python
from contextlib import ExitStack

import numpy as np

import concourse.bass as bass
from concourse import mybir

ALU = mybir.AluOpType
ACT = mybir.ActivationFunctionType
AX = mybir.AxisListType
F32 = mybir.dt.float32
F16 = mybir.dt.float16
BF16 = mybir.dt.bfloat16
I32 = mybir.dt.int32
RMAX = bass.bass_isa.ReduceOp.max
RADD = bass.bass_isa.ReduceOp.add

P = 128
NBATCH = 16
SEQ = 256
E = 256
HID = 1024
HEADS = 16
HD = E // HEADS
NT = SEQ // P
NC = E // P
W = NT * E
CHUNKS = HID // P
ROUNDS = CHUNKS // 2
SLOTS = HEADS // 2
STK = 4 * HD
VW = 2 * HD + 1

X_SCALE = 2.0 ** 11
W_SCALE = 2.0 ** 14
Q_SCALE = 2.0 ** 6
QKV_OUT = Q_SCALE / (X_SCALE * W_SCALE)
LN_EPS = 1e-5
QUANT_EPS = 1e-8
MASKED = -1.5 * 2.0 ** 127

MISC = [
    ("norm2", 0, "a", 1), ("qk0", 0, "b", 1), ("qk1", 1, "a", 1), ("attn_t", 1, "b", 3),
    ("out_proj", 2, "a", 3), ("v", 2, "b", 1), ("norm3", 3, "b", 3), ("stack_q0", 5, "a", 1),
    ("stack_k0", 5, "b", 1), ("stack_q1", 6, "a", 1), ("stack_k1", 6, "b", 1), ("norm1", 7, "a", -1),
]
STACK_DVE = ("stack_k0", "stack_q0", "stack_q1")

PE_SLOT = ["scores", "product_v", "misc_a", "transpose_0", "up", "gate", "transpose_1", "misc_b",
           "down"]
PE_OTHER = {
    0: ["misc_a", "scores", "product_v", "transpose_0", "up", "gate", "transpose_1", "misc_b", "down"],
    3: ["scores", "product_v", "misc_a", "transpose_0", "up", "gate", "transpose_1", "down", "misc_b"],
    6: ["scores", "product_v", "transpose_0", "up", "misc_a", "gate", "transpose_1", "misc_b", "down"],
}
ACT_SLOT = ["misc_a", "prob_hi_0", "tanh", "exps_0", "prob_hi_1", "exps_1", "misc_b", "hidden_hi"]
ACT_OTHER = {
    1: ["misc_a", "prob_hi_0", "tanh", "exps_0", "prob_hi_1", "misc_b", "exps_1", "hidden_hi"],
    2: ["misc_a", "prob_hi_0", "tanh", "exps_0", "exps_1", "prob_hi_1", "misc_b", "hidden_hi"],
    3: ["prob_hi_0", "misc_a", "exps_1", "tanh", "exps_0", "prob_hi_1", "misc_b", "hidden_hi"],
    4: ["prob_hi_0", "misc_a", "tanh", "exps_0", "exps_1", "prob_hi_1", "hidden_hi", "misc_b"],
    5: ["prob_hi_0", "misc_a", "tanh", "exps_0", "prob_hi_1", "exps_1", "misc_b", "hidden_hi"],
    7: ["misc_a", "prob_hi_0", "tanh", "misc_b", "exps_0", "prob_hi_1", "exps_1", "hidden_hi"],
}
ACT_EXTRA = {
    (3, "hidden_hi"): "rope_hi_0", (4, "hidden_hi"): "rope_hi_1",
}
DVE_SLOT = ["row_max", "pv_inverse", "exp_biases", "pv_add", "misc_a", "pv_scale", "silu", "hidden",
            "prob_lo_1", "misc_b"]
DVE_OTHER = {
    1: ["pv_inverse", "row_max", "exp_biases", "pv_add", "misc_a", "pv_scale", "silu", "hidden", "prob_lo_1",
        "misc_b"],
    4: ["row_max", "pv_inverse", "exp_biases", "misc_a", "pv_add", "pv_scale", "silu", "hidden", "prob_lo_1",
        "misc_b"],
}
DVE_EXTRA = {
    (1, "pv_inverse"): ["ffn_added"], (2, "pv_scale"): ["rows_3"], (2, "prob_lo_1"): ["stats_3"],
    (3, "row_max"): ["stats_wait_3"], (3, "pv_inverse"): ["mean_3"], (3, "exp_biases"): ["var_3"],
    (3, "misc_a"): ["apply_3"], (5, "exp_biases"): ["ffn_added"], (5, "pv_add"): ["rows_1", "stats_1"],
    (5, "pv_scale"): ["stats_wait_1"], (5, "silu"): ["mean_1", "var_1"], (6, "exp_biases"): ["rows_2"],
    (6, "pv_add"): ["stats_2"], (6, "misc_a"): ["stats_wait_2"], (6, "pv_scale"): ["mean_2"],
    (6, "silu"): ["var_2"],
}
POOL_SLOT = [
    ["prob_lo", "hidden_lo"],
    ["mul_0", "prob_lo", "hidden_lo"],
    ["add_0", "mul_1", "prob_lo", "hidden_lo"],
    ["pow_3", "add_1", "prob_lo", "hidden_lo"],
    ["prob_lo", "lo_00", "lo_01", "hidden_lo"],
    ["lo_10", "lo_11", "prob_lo", "pow_1", "hidden_lo"],
    ["apply_1", "prob_lo", "pow_2", "hidden_lo"],
    ["apply_2", "prob_lo", "hidden_lo"],
]
FIRST_STEP = -1
LOOP_FROM, LOOP_TO = 4, 14
LAST_STEP = NBATCH + 3


def live(b):
    return 0 <= b < NBATCH


def misc_before(t, name):
    index = [m[0] for m in MISC].index(name)
    done = sum(live(u - lag) for u in range(FIRST_STEP, t) for _, _, _, lag in MISC)
    return done + sum(live(t - lag) for _, _, _, lag in MISC[:index])


def misc_through(t, name):
    return misc_before(t, name) + 1


def misc_uses(slot, place):
    return [(name, lag) for name, s, p, lag in MISC if (s, p) == (slot, place)]


def rounds_before(t, slot):
    done = sum(ROUNDS * (live(u) + live(u - 3)) for u in range(0, t))
    return done + (min(slot, ROUNDS) * live(t)) + (max(slot - ROUNDS, 0) * live(t - 3))


class Step:

    def __init__(self, first, i=None):
        self.first, self.i = first, i
        self.parity = first % 2

    def live(self, lag):
        return live(self.first - lag)

    def at(self, count, least=1):
        a = count(self.first)
        if self.i is None:
            return max(a, 0)
        slope = count(self.first + 2) - a
        assert count(self.first + 4) - a == 2 * slope and a >= least
        return self.i * slope + a


def run_steps(engine, body, before={}):
    for t in range(FIRST_STEP, LOOP_FROM):
        if t in before:
            before[t]()
        body(Step(t))
    with engine.Fori(0, (LOOP_TO - LOOP_FROM) // 2) as i:
        body(Step(LOOP_FROM, i))
        body(Step(LOOP_FROM + 1, i))
    for t in range(LOOP_TO, LAST_STEP + 1):
        body(Step(t))


def macaron_kernel(nc, x, wqkvo, w_up_t, w_gate_t, w_down_t, ident, mask, rope_cos, rope_sin, out):
    with ExitStack() as ctx:
        def sb(name, shape, dt=F32):
            return ctx.enter_context(nc.sbuf_tensor(name, shape, dt))

        def ps(name, shape, dt=F32):
            return ctx.enter_context(nc.psum_tensor(name, shape, dt))

        def sem(name):
            return ctx.enter_context(nc.semaphore(name))

        ident_f = sb("ident_f", [P, P])
        ident_h = sb("ident_h", [P, P], F16)
        ident_b = sb("ident_b", [P, P], BF16)
        mask_f = sb("mask_f", [P, 2 * P])
        mask_b = sb("mask_b", [P, 2 * P], BF16)
        cos = sb("cos", [P, NT, 2 * E])
        sin = sb("sin", [P, NT, 2 * E])
        raw_up = sb("raw_up", [P, NC * HID])
        raw_gate = sb("raw_gate", [P, NC * HID])
        raw_down = sb("raw_down", [P, CHUNKS * E])
        raw_w = sb("raw_w", [P, NC, 4, E])
        tern_up = sb("tern_up", [P, NC, HID], F16)
        tern_gate = sb("tern_gate", [P, NC, HID], F16)
        tern_down = sb("tern_down", [P, CHUNKS, E], F16)
        below = sb("below", [P, NC * HID], F16)
        w_hi = sb("w_hi", [P, NC, 4, E], F16)
        w_lo = sb("w_lo", [P, NC, 4, E], F16)
        w_absmax = sb("w_absmax", [P, NC * 4])
        w_max = sb("w_max", [P, 4])
        w_max_all = sb("w_max_all", [P, 4])
        w_pow = sb("w_pow", [P, 4])
        w_inv = sb("w_inv", [P, 4])
        w_mul = sb("w_mul", [P, 4])
        abs_sum = sb("abs_sum", [P, 4])
        abs_sum_all = sb("abs_sum_all", [P, 4])
        tern_scale = sb("tern_scale", [P, 4])
        thr_hi = sb("thr_hi", [P, 4])
        thr_lo = sb("thr_lo", [P, 4])
        scale_prod = sb("scale_prod", [P, 4])
        tanh_scale = sb("tanh_scale", [P, 1])
        down_scale = sb("down_scale", [P, 1])
        exp_scale = sb("exp_scale", [P, 1])
        neg_exp_scale = sb("neg_exp_scale", [P, 1])
        proj_scale = sb("proj_scale", [P, 1])
        minus_half = sb("minus_half", [P, NT])

        xs = sb("xs", [P, NBATCH * W])

        stats = {k: sb(f"stats{k}", [P, NT, 6]) for k in (1, 2, 3)}
        mv = {k: sb(f"mv{k}", [P, NT, 2]) for k in (1, 2, 3)}
        var_s = {k: sb(f"var_s{k}", [P, NT]) for k in (1, 2, 3)}
        rstd = {k: sb(f"rstd{k}", [P, NT]) for k in (1, 2, 3)}
        centred = {k: sb(f"centred{k}", [P, NT, E]) for k in (1, 2)}
        xhat = {k: sb(f"xhat{k}", [P, NT, E]) for k in (1, 2, 3)}
        xt_hi = {k: sb(f"xt_hi{k}", [P, NC, SEQ], F16) for k in (1, 2, 3)}
        xt_lo = {k: sb(f"xt_lo{k}", [P, NC, SEQ], F16) for k in (1, 2, 3)}

        tanh_b = sb("tanh_b", [P, 512])
        silu_b = sb("silu_b", [P, 512])
        hid = sb("hid", [P, 2, 512])
        hid_h = sb("hid_h", [P, 2, 2, SEQ], F16)
        hid_l = sb("hid_l", [P, 2, 2, SEQ], F16)

        qk_rows = sb("qk_rows", [P, NT, 2 * E])
        rope_c = sb("rope_c", [P, NT, 2 * E])
        rope_s = sb("rope_s", [P, NT, 2 * E])
        rope_r = sb("rope_r", [P, NT, 2 * E])
        q_row = sb("q_row", [P, NT, HEADS, 4, HD], F16)
        k_row = sb("k_row", [P, NT, HEADS, 4, HD], F16)
        q_stk = sb("q_stk", [P, 2, SLOTS, SEQ], F16)
        k_stk = sb("k_stk", [P, 2, SLOTS, SEQ], F16)
        v_row = sb("v_row", [P, 2, NT * HEADS, VW], F16)

        neg_max = sb("neg_max", [P, 4])
        exp_bias = sb("exp_bias", [P, 4])
        prob = sb("prob", [P, 2, 2, 384])
        prob_t = sb("prob_t", [P, 2, 384])
        prob_h = sb("prob_h", [P, 2, 2, 384], F16)
        prob_l = sb("prob_l", [P, 2, 2, 384], F16)
        inv_sum = sb("inv_sum", [P, NT, 2, 1])
        pv_sum = sb("pv_sum", [P, NT, 2, HD])
        attn = sb("attn", [P, NT, E])
        attn_h = sb("attn_h", [P, NC, SEQ], F16)
        attn_l = sb("attn_l", [P, NC, SEQ], F16)

        up_ps = ps("up_ps", [P, 512])
        gate_ps = ps("gate_ps", [P, 512])
        down_ps = ps("down_ps", [P, 512])
        score_ps = ps("score_ps", [P, 2, 512])
        probt_ps = ps("probt_ps", [P, 512])
        pv_ps = ps("pv_ps", [P, 512])
        misc_ps = ps("misc_ps", [P, 512])
        misc_h16 = misc_ps[:, :].bitcast(F16)

        x_loaded = [sem("x_even_loaded"), sem("x_odd_loaded")]
        up_loaded, gate_loaded, down_loaded = sem("up_loaded"), sem("gate_loaded"), sem("down_loaded")
        w_loaded, ident_loaded, mask_loaded = sem("w_loaded"), sem("ident_loaded"), sem("mask_loaded")
        rope_loaded, out_stored = sem("rope_loaded"), sem("out_stored")
        abs_done, abs_all, tern_done = sem("abs_done"), sem("abs_all"), sem("tern_done")
        wmax_done, wmax_all, split_done = sem("wmax_done"), sem("wmax_all"), sem("split_done")
        casts_done, ones_done = sem("casts_done"), sem("ones_done")
        scales_done, w_scales_done = sem("scales_done"), sem("w_scales_done")
        below_done = sem("below_done")
        misc_written, scores_done, probt_done = sem("misc_written"), sem("scores_done"), sem("probt_done")
        pv_done, up_done, gate_done = sem("pv_done"), sem("up_done"), sem("gate_done")
        down_done = sem("down_done")
        misc_taken = sem("misc_taken")
        stats_done = {k: sem(f"stats_done{k}") for k in (1, 2, 3)}
        mean_done = {k: sem(f"mean_done{k}") for k in (1, 2, 3)}
        var_done = {k: sem(f"var_done{k}") for k in (1, 2, 3)}
        rstd_done = {k: sem(f"rstd_done{k}") for k in (1, 2, 3)}
        centred_done = {k: sem(f"centred_done{k}") for k in (1, 2)}
        xhat_done = {k: sem(f"xhat_done{k}") for k in (1, 2, 3)}
        xt_hi_done = {k: sem(f"xt_hi_done{k}") for k in (1, 2, 3)}
        tanh_done, silu_done, hid_done = sem("tanh_done"), sem("silu_done"), sem("hid_done")
        hid_h_done, hid_l_done = sem("hid_h_done"), sem("hid_l_done")
        rope_mul_done = sem("rope_mul_done")
        rope_done, row_hi_done = sem("rope_done"), sem("row_hi_done")
        row_lo_done = [[sem(f"{m}_lo_done{tile}") for tile in range(NT)] for m in "qk"]
        v_hi_done = sem("v_hi_done")
        max_done, bias_done = sem("max_done"), sem("bias_done")
        exp_done = [sem("exp_done0"), sem("exp_done1")]
        prob_h_done, prob_t_done = sem("prob_h_done"), sem("prob_t_done")
        prob_l_done = [sem("prob_l_done0"), sem("prob_l_done1")]
        inv_done, pv_sum_done, attn_done = sem("inv_done"), sem("pv_sum_done"), sem("attn_done")
        attn_h_done = sem("attn_h_done")
        ffn1_added, ffn2_added = sem("ffn1_added"), sem("ffn2_added")

        def x_rows(st, lag, lo=0, n=W):
            return xs[:, bass.ds(st.at(lambda t: (t - lag) * W + lo, least=0), n)]

        def copy_stack(engine, st, name, lag, copy):
            tile = int(name[-1])
            stk = q_stk if name.startswith("stack_q") else k_stk
            engine.wait_ge(misc_written, st.at(lambda t: misc_through(t, name)))
            copy(stk[:, (st.first - lag) % 2, :, tile * P:(tile + 1) * P],
                 misc_h16[:, :].rearrange("p (s n) -> p s n", n=P)).then_inc(misc_taken, 1)

        def row_lo(engine, st, tile, m):
            if not st.live(1):
                return
            row, places = ((q_row, slice(1, 3)), (k_row, slice(1, 4, 2)))[m]
            r = rope_r[:, tile, :].rearrange("p (m h d) -> p m h d", m=2, d=HD)[:, m]
            engine.wait_ge(row_hi_done, st.at(lambda t: 4 * (t - 1) + 2 * tile + m + 1))
            engine.tensor_tensor(row[:, tile, :, places, :], r[:, :, None, :].to_broadcast([P, HEADS, 2, HD]),
                                 row[:, tile, :, 0:1, :].to_broadcast([P, HEADS, 2, HD]), ALU.subtract
                                 ).then_inc(row_lo_done[m][tile], 1)

        x_dram = x.rearrange("b (n p) e -> b p n e", p=P)
        out_dram = out.rearrange("b (n p) e -> b p n e", p=P)

        block = ctx.enter_context(nc.Block())

        @block.sync
        def _(sp):
            def rows(b):
                return xs[:, bass.ds(b * W, W)].rearrange("p (n e) -> p n e", n=NT)

            sp.dma_start(rows(0), x_dram[0]).then_inc(x_loaded[0], 16)
            sp.dma_start(raw_up[:, :], w_up_t).then_inc(up_loaded, 16)
            sp.dma_start(raw_down[:, :], w_down_t).then_inc(down_loaded, 16)
            sp.dma_start(rows(1), x_dram[1]).then_inc(x_loaded[1], 16)
            sp.dma_start(cos[:, :, :], rope_cos).then_inc(rope_loaded, 16)
            sp.dma_start(sin[:, :, :], rope_sin).then_inc(rope_loaded, 16)
            with sp.Fori(1, NBATCH // 2) as i:
                for b in range(2):
                    sp.wait_ge(x_loaded[b], i * 16)
                    sp.dma_start(xs[:, bass.ds(i * (2 * W) + b * W, W)].rearrange("p (n e) -> p n e", n=NT),
                                 x_dram[bass.ds(i * 2 + b, 1)].rearrange("o p n e -> (o p) n e")
                                 ).then_inc(x_loaded[b], 16)
            with sp.Fori(0, NBATCH) as b:
                sp.wait_ge(ffn2_added, b + 1)
                sp.dma_start(out_dram[bass.ds(b, 1)].rearrange("o p n e -> (o p) n e"),
                             xs[:, bass.ds(b * W, W)].rearrange("p (n e) -> p n e", n=NT)
                             ).then_inc(out_stored, 16)
            sp.wait_ge(out_stored, 16 * NBATCH)

        @block.tensor
        def _(pe):
            def split_product(dst, pairs, flags):
                for n, (lhs, rhs) in enumerate(pairs):
                    mm = pe.matmul(dst, lhs, rhs, start=flags and n == 0, stop=n == len(pairs) - 1,
                                   skip_group_check=True)
                return mm

            def three(a_hi, a_lo, b_hi, b_lo):
                return [(a_hi, b_hi), (a_hi, b_lo), (a_lo, b_hi)]

            def scores(st, s):
                pe.wait_ge(misc_taken, st.at(lambda t: misc_through(t - 1, "stack_k1")))
                par = st.parity
                for j in range(2):
                    pe.wait_ge(exp_done[j], st.at(lambda t: SLOTS * (t - 2) + s))
                    pe.matmul(score_ps[:, j, P:3 * P], ident_b[:, :], mask_b[:, :], start=True, stop=False,
                              skip_group_check=True)
                    q = q_stk[STK * j:STK * (j + 1), par, s, :]
                    k = k_stk[STK * j:STK * (j + 1), par, s, :]
                    pe.matmul(score_ps[:, j, 0:2 * P], q[:, P:2 * P], k[:, 0:2 * P], start=False, stop=True,
                              skip_group_check=True)
                    mm = pe.matmul(score_ps[:, j, 2 * P:3 * P], q[:, 0:P], k[:, 0:P], start=False, stop=True,
                                   skip_group_check=True)
                mm.then_inc(scores_done, 1)

            def pair_of(s, back):
                return (2, s - back) if s >= back else (3, s - back + SLOTS)

            def product_v(st, s):
                lag, pair = pair_of(s, 2)
                if not st.live(lag):
                    return
                for j in range(2):
                    pe.wait_ge(prob_l_done[j], st.at(lambda t: SLOTS * (t - lag) + pair + 1))
                pe.wait_ge(pv_sum_done, st.at(lambda t: SLOTS * (t - lag) + pair))
                v = v_row[:, (st.first - lag) % 2, :, :].rearrange("p (n h) w -> p n h w", n=NT)
                first = True
                for j in range(2):
                    h = 2 * pair + j
                    for tile, blocks in ((0, [(0, 0)]), (1, [(1, 0), (2, 1)])):
                        dst = pv_ps[:, (2 * tile + j) * VW:(2 * tile + j + 1) * VW]
                        for col, keys in blocks:
                            for part in (prob_h, prob_l):
                                mm = pe.matmul(dst, part[:, pair % 2, j, col * P:(col + 1) * P], v[:, keys, h, :],
                                               start=first, stop=True, skip_group_check=True)
                                first = False
                mm.then_inc(pv_done, 1)

            def transpose_probs(st, s, j):
                lag, pair = pair_of(s, 1)
                if not st.live(lag):
                    return
                pe.wait_ge(exp_done[j], st.at(lambda t: SLOTS * (t - lag) + pair + 1))
                if j == 0:
                    pe.wait_ge(prob_l_done[1], st.at(lambda t: SLOTS * (t - lag) + pair))
                else:
                    pe.wait_ge(prob_t_done, st.at(lambda t: SLOTS * (t - lag) + pair + 1))
                for n, col in enumerate((2, 0, 1)):
                    mm = pe.transpose(probt_ps[:, n * P:(n + 1) * P], prob[:, pair % 2, j, col * P:(col + 1) * P],
                                      ident_f[:, :])
                mm.then_inc(probt_done, 1)

            def up_gate(st, s, dst, tern, done, read):
                k, lag, r = (1, 0, s) if s < ROUNDS else (3, 3, s - ROUNDS)
                if not st.live(lag):
                    return
                if st.first == 0 and s == 0:
                    pe.wait_ge(tern_done, 1 if dst is up_ps else 2)
                pe.wait_ge(misc_taken, st.at(
                    lambda t: misc_through(t - 1, "norm1") if k == 1 else misc_through(t, "norm3")))
                pe.wait_ge(read, st.at(lambda t: rounds_before(t, s)))
                for m in range(2):
                    at = (2 * r + m) * P
                    pairs = [(tern[:, c, at:at + P], part[:, c, :]) for c in range(NC)
                             for part in (xt_hi[k], xt_lo[k])]
                    mm = split_product(dst[:, m * SEQ:(m + 1) * SEQ], pairs, m == 0)
                mm.then_inc(done, 1)

            def down(st, s):
                lag, r = [(4, 3), (0, 0), (0, 1), (0, 2), (0, 3), (3, 0), (3, 1), (3, 2)][s]
                if not st.live(lag):
                    return
                if st.first == 0 and s == 1:
                    pe.wait_ge(tern_done, 3)
                pe.wait_ge(hid_l_done, st.at(lambda t: rounds_before(t, s)))
                if r == 0:
                    if lag == 0:
                        pe.wait_ge(ffn2_added, st.at(lambda t: t - 3))
                    else:
                        pe.wait_ge(ffn1_added, st.at(lambda t: min(t + 1, NBATCH)))
                par = r % 2
                for tile in range(NT):
                    pairs = [(part[:, par, m, tile * P:(tile + 1) * P], tern_down[:, 2 * r + m, :])
                             for m in range(2) for part in (hid_h, hid_l)]
                    mm = split_product(down_ps[:, tile * E:(tile + 1) * E], pairs, r == 0 and tile == 0)
                mm.then_inc(down_done, 1)

            def transpose_rows(src):
                for c in range(NC):
                    for tile in range(NT):
                        mm = pe.transpose(misc_ps[:, c * SEQ + tile * P:c * SEQ + (tile + 1) * P],
                                          src[:, tile, c * P:(c + 1) * P], ident_f[:, :])
                return mm

            def misc(st, s, place):
                for name, lag in misc_uses(s, place):
                    if not st.live(lag):
                        continue
                    pe.wait_ge(misc_taken, st.at(lambda t: misc_before(t, name)))
                    if name.startswith("norm"):
                        k = int(name[-1])
                        pe.wait_ge(xhat_done[k], st.at(lambda t: t - lag + 1))
                        mm = transpose_rows(xhat[k])
                    elif name in ("qk0", "qk1"):
                        tile = int(name[-1])
                        pe.wait_ge(split_done, 8)
                        rows = slice(tile * P, (tile + 1) * P)
                        pairs = [p for c in range(NC) for p in three(
                            xt_hi[2][:, c, rows], xt_lo[2][:, c, rows],
                            w_hi[:, c, 0:2, :].rearrange("p m e -> p (m e)"),
                            w_lo[:, c, 0:2, :].rearrange("p m e -> p (m e)"))]
                        mm = split_product(misc_ps[:, :], pairs, True)
                    elif name == "v":
                        for tile in range(NT):
                            rows = slice(tile * P, (tile + 1) * P)
                            pairs = [p for c in range(NC) for p in three(
                                xt_hi[2][:, c, rows], xt_lo[2][:, c, rows], w_hi[:, c, 2, :], w_lo[:, c, 2, :])]
                            mm = split_product(misc_ps[:, tile * E:(tile + 1) * E], pairs, tile == 0)
                    elif name == "attn_t":
                        pe.wait_ge(attn_done, st.at(lambda t: SLOTS * (t - lag + 1)))
                        mm = transpose_rows(attn)
                    elif name == "out_proj":
                        for tile in range(NT):
                            rows = slice(tile * P, (tile + 1) * P)
                            pairs = [p for c in range(NC) for p in three(
                                attn_h[:, c, rows], attn_l[:, c, rows], w_hi[:, c, 3, :], w_lo[:, c, 3, :])]
                            mm = split_product(misc_ps[:, tile * E:(tile + 1) * E], pairs, tile == 0)
                    else:
                        tile = int(name[-1])
                        row = q_row if name.startswith("stack_q") else k_row
                        pe.wait_ge(row_lo_done[int(row is k_row)][tile], st.at(lambda t: t - lag + 1))
                        for pair in range(SLOTS):
                            mm = pe.transpose(misc_h16[:, pair * P:(pair + 1) * P],
                                              row[:, tile, 2 * pair:2 * pair + 2, :, :].rearrange("p h s d -> p (h s d)"),
                                              ident_h[:, :])
                    mm.then_inc(misc_written, 1)

            def step(st):
                for s in range(SLOTS):
                    for what in PE_OTHER.get(s, PE_SLOT):
                        if what == "scores" and st.live(2):
                            scores(st, s)
                        elif what == "product_v":
                            product_v(st, s)
                        elif what.startswith("misc"):
                            misc(st, s, what[-1])
                        elif what.startswith("transpose"):
                            transpose_probs(st, s, int(what[-1]))
                        elif what == "up":
                            up_gate(st, s, up_ps, tern_up, up_done, silu_done)
                        elif what == "gate":
                            up_gate(st, s, gate_ps, tern_gate, gate_done, hid_done)
                        elif what == "down":
                            down(st, s)

            pe.wait_ge(ident_loaded, 16)
            run_steps(pe, step, before={1: lambda: pe.wait_ge(casts_done, 4)})

        @block.scalar
        def _(act):
            def set_up_loads():
                act.dma_start(ident_f[:, :], ident).then_inc(ident_loaded, 16)
                act.dma_start(raw_gate[:, :], w_gate_t).then_inc(gate_loaded, 16)
                act.dma_start(mask_f[:, :], mask).then_inc(mask_loaded, 16)
                act.dma_start(raw_w[:, :, :, :], wqkvo).then_inc(w_loaded, 16)

            def sum_weights():
                for n, (raw, junk, loaded) in enumerate((
                        (raw_up, tern_up, up_loaded), (raw_gate, tern_gate, gate_loaded))):
                    act.wait_ge(loaded, 16)
                    act.activation(junk[:, :, :].rearrange("p a b -> p (a b)"), raw[:, :], ACT.Abs,
                                   accum_out=abs_sum[:, n:n + 1]).then_inc(abs_done, 1)

            def split_misc(st, name, lag, dst, done):
                act.wait_ge(misc_written, st.at(lambda t: misc_through(t, name)))
                act.activation(dst[:, :, :].rearrange("p c n -> p (c n)"), misc_ps[:, :], ACT.Copy).then_inc(done, 1)

            def misc(st, s, place):
                for name, lag in misc_uses(s, place):
                    if not st.live(lag):
                        continue
                    if name.startswith("norm"):
                        k = int(name[-1])
                        split_misc(st, name, lag, xt_hi[k], xt_hi_done[k])
                    elif name == "attn_t":
                        split_misc(st, name, lag, attn_h, attn_h_done)
                    elif name in ("qk0", "qk1"):
                        act.wait_ge(misc_written, st.at(lambda t: misc_through(t, name)))
                        act.activation(qk_rows[:, int(name[-1]), :], misc_ps[:, :], ACT.Copy).then_inc(misc_taken, 1)
                    elif name == "v":
                        act.wait_ge(ones_done, 1)
                        act.wait_ge(misc_written, st.at(lambda t: misc_through(t, name)))
                        act.activation(v_row[:, (st.first - lag) % 2, :, 0:HD],
                                       misc_ps[:, :].rearrange("p (m d) -> p m d", d=HD), ACT.Copy,
                                       scale=QKV_OUT).then_inc(v_hi_done, 1)
                    elif name.startswith("stack") and name not in STACK_DVE:
                        copy_stack(act, st, name, lag, lambda dst, src: act.activation(dst, src, ACT.Copy))

            def rope_hi(st, tile):
                if not st.live(1):
                    return
                act.wait_ge(rope_done, st.at(lambda t: 2 * (t - 1) + tile + 1))
                r = rope_r[:, tile, :].rearrange("p (m h d) -> p m h d", m=2, d=HD)
                for m, (row, places) in enumerate(((q_row, slice(0, 4, 3)), (k_row, slice(0, 4, 2)))):
                    dst = row[:, tile, :, places, :]
                    src = r[:, m, :, None, :].to_broadcast([P, HEADS, 2, HD])
                    act.activation(dst, src, ACT.Copy).then_inc(row_hi_done, 1)

            def prob_hi(st, s, j):
                lag, pair = (2, s - 1) if s else (3, SLOTS - 1)
                if not st.live(lag):
                    return
                act.wait_ge(probt_done, st.at(lambda t: 2 * (SLOTS * (t - lag) + pair) + j + 1))
                act.activation(prob_h[:, pair % 2, j, :], probt_ps[:, 0:384], ACT.Copy).then_inc(prob_h_done, 1)
                if j == 0:
                    act.wait_ge(prob_l_done[0], st.at(lambda t: SLOTS * (t - lag) + pair - 1))
                    act.activation(prob_t[:, pair % 2, :], probt_ps[:, 0:384], ACT.Copy).then_inc(prob_t_done, 1)

            def exps(st, s, j):
                act.wait_ge(bias_done, st.at(lambda t: SLOTS * (t - 2) + s + 1))
                act.activation(prob[:, s % 2, j, 0:256], score_ps[:, j, 0:256], ACT.Exp,
                               bias=exp_bias[:, j:j + 1], scale=exp_scale[:, :])
                act.activation(prob[:, s % 2, j, 256:384], score_ps[:, j, 256:384], ACT.Exp,
                               bias=exp_bias[:, 2 + j:3 + j], scale=exp_scale[:, :]).then_inc(exp_done[j], 1)

            def tanh(st, s):
                if not st.live(0 if s < ROUNDS else 3):
                    return
                act.wait_ge(up_done, st.at(lambda t: rounds_before(t, s) + 1))
                act.activation(tanh_b[:, :], up_ps[:, :], ACT.Tanh, scale=tanh_scale[:, :]).then_inc(tanh_done, 1)

            def hidden_hi(st, s):
                if not st.live(0 if s < ROUNDS else 3):
                    return
                act.wait_ge(hid_done, st.at(lambda t: rounds_before(t, s) + 1))
                act.activation(hid_h[:, s % 2, :, :].rearrange("p m n -> p (m n)"), hid[:, s % 2, :],
                               ACT.Copy).then_inc(hid_h_done, 1)

            def step(st):
                for s in range(SLOTS):
                    for what in ACT_OTHER.get(s, ACT_SLOT):
                        if (s, what) in ACT_EXTRA:
                            rope_hi(st, int(ACT_EXTRA[s, what][-1]))
                        if what.startswith("misc"):
                            misc(st, s, what[-1])
                        elif what.startswith("prob_hi"):
                            prob_hi(st, s, int(what[-1]))
                        elif what.startswith("exps") and st.live(2):
                            exps(st, s, int(what[-1]))
                        elif what == "tanh":
                            tanh(st, s)
                        elif what == "hidden_hi":
                            hidden_hi(st, s)

            set_up_loads()
            sum_weights()
            run_steps(act, step, before={0: lambda: act.wait_ge(scales_done, 4)})

        @block.vector
        def _(dve):
            def set_up_constants():
                dve.memset(minus_half[:, :], -0.5).then_inc(casts_done, 1)
                dve.memset(v_row[:, :, :, 2 * HD:VW], 1.0).then_inc(ones_done, 1)

            def set_up_casts():
                dve.wait_ge(ident_loaded, 16)
                dve.tensor_copy(ident_h[:, :], ident_f[:, :]).then_inc(casts_done, 1)
                dve.wait_ge(mask_loaded, 16)
                dve.tensor_copy(mask_b[:, :], mask_f[:, :]).then_inc(casts_done, 1)
                dve.tensor_copy(ident_b[:, :], ident_f[:, :]).then_inc(casts_done, 1)

            def set_up_ternary():
                def scales(m):
                    dve.tensor_scalar(tern_scale[:, m], abs_sum_all[:, m], 1.0 / (E * HID), QUANT_EPS,
                                      ALU.mult, ALU.add).then_inc(scales_done, 1)

                def thresholds(m):
                    dve.tensor_scalar(thr_hi[:, m], tern_scale[:, m], 0.5, None, ALU.mult).then_inc(scales_done, 1)
                    dve.tensor_scalar(thr_lo[:, m], tern_scale[:, m], -0.5, None, ALU.mult).then_inc(scales_done, 1)

                def ternary(n, raw, tern):
                    if n:
                        dve.wait_ge(tern_done, n)
                    dve.tensor_scalar(below[:, :], raw[:, :], thr_lo[:, n:n + 1], None, ALU.is_lt
                                      ).then_inc(below_done, 1)
                    dve.wait_ge(below_done, n + 1)
                    dve.scalar_tensor_tensor(out=tern[:, :, :].rearrange("p a b -> p (a b)"), in0=raw[:, :],
                                             scalar=thr_hi[:, n:n + 1], in1=below[:, :], op0=ALU.is_gt,
                                             op1=ALU.subtract).then_inc(tern_done, 1)

                dve.wait_ge(abs_all, 1)
                scales(slice(0, 2))
                dve.wait_ge(scales_done, 1)
                thresholds(slice(0, 2))
                dve.tensor_scalar(tanh_scale[:, :], tern_scale[:, 0:1], 0.5 / X_SCALE, None, ALU.mult
                                  ).then_inc(scales_done, 1)
                dve.tensor_tensor(scale_prod[:, 0:1], tern_scale[:, 0:1], tern_scale[:, 1:2], ALU.mult
                                  ).then_inc(scales_done, 1)
                dve.wait_ge(scales_done, 5)
                ternary(0, raw_up, tern_up)
                ternary(1, raw_gate, tern_gate)
                dve.wait_ge(down_loaded, 16)
                dve.tensor_reduce(abs_sum[:, 2:3], raw_down[:, :], AX.X, ALU.add, apply_absolute_value=True
                                  ).then_inc(abs_done, 1)
                dve.wait_ge(abs_all, 2)
                scales(slice(2, 3))
                dve.wait_ge(scales_done, 6)
                thresholds(slice(2, 3))
                dve.tensor_tensor(down_scale[:, :], scale_prod[:, 0:1], tern_scale[:, 2:3], ALU.mult
                                  ).then_inc(scales_done, 1)
                dve.wait_ge(scales_done, 9)
                ternary(2, raw_down, tern_down)

            def weight_maxima():
                dve.wait_ge(w_loaded, 16)
                dve.tensor_reduce(w_absmax[:, :], raw_w[:, :, :, :].rearrange("p c m e -> p (c m) e"), AX.X, ALU.max,
                                  apply_absolute_value=True).then_inc(w_scales_done, 1)
                dve.wait_ge(w_scales_done, 1)
                dve.tensor_tensor(w_max[:, :], w_absmax[:, 0:4], w_absmax[:, 4:8], ALU.max).then_inc(wmax_done, 1)

            def weight_powers():
                dve.wait_ge(wmax_all, 1)
                dve.tensor_scalar(w_max[:, :], w_max_all[:, :], 1e-30, None, ALU.max).then_inc(w_scales_done, 1)
                dve.wait_ge(w_scales_done, 2)
                dve.tensor_scalar(w_pow[:, :].bitcast(I32), w_max[:, :].bitcast(I32), 0x7F800000, None,
                                  ALU.bitwise_and).then_inc(w_scales_done, 1)
                dve.wait_ge(w_scales_done, 3)
                dve.reciprocal(w_inv[:, :], w_pow[:, :]).then_inc(w_scales_done, 1)
                dve.tensor_tensor(scale_prod[:, 1:2], w_pow[:, 0:1], w_pow[:, 1:2], ALU.mult).then_inc(w_scales_done, 1)
                dve.tensor_tensor(scale_prod[:, 2:3], w_pow[:, 2:3], w_pow[:, 3:4], ALU.mult).then_inc(w_scales_done, 1)
                dve.wait_ge(w_scales_done, 6)
                dve.tensor_scalar(w_mul[:, :], w_inv[:, :], W_SCALE, None, ALU.mult).then_inc(w_scales_done, 1)
                to_scores = 1.0 / (Q_SCALE * Q_SCALE * HD ** 0.5)
                dve.tensor_scalar(neg_exp_scale[:, :], scale_prod[:, 1:2], -to_scores, None, ALU.mult
                                  ).then_inc(w_scales_done, 1)
                dve.tensor_scalar(proj_scale[:, :], scale_prod[:, 2:3], 1.0 / (Q_SCALE * W_SCALE), None, ALU.mult
                                  ).then_inc(w_scales_done, 1)
                dve.tensor_scalar(exp_scale[:, :], scale_prod[:, 1:2], to_scores, None, ALU.mult).then_inc(w_scales_done, 1)
                dve.wait_ge(w_scales_done, 10)

            def split_weights_hi():
                for m in range(4):
                    dve.tensor_scalar(w_hi[:, :, m, :], raw_w[:, :, m, :], w_mul[:, m:m + 1], None, ALU.mult
                                      ).then_inc(split_done, 1)

            def split_weights_lo():
                for m in range(4):
                    dve.wait_ge(split_done, m + 1)
                    dve.scalar_tensor_tensor(out=w_lo[:, :, m, :], in0=raw_w[:, :, m, :], scalar=w_mul[:, m:m + 1],
                                             in1=w_hi[:, :, m, :], op0=ALU.mult, op1=ALU.subtract
                                             ).then_inc(split_done, 1)

            def wait_norm_rows(st, k, lag):
                if not st.live(lag):
                    return
                if k == 1:
                    dve.wait_ge(x_loaded[(st.first - lag) % 2], st.at(lambda t: 16 * ((t - lag) // 2) + 16))
                elif k == 2:
                    dve.wait_ge(ffn1_added, st.at(lambda t: t - lag + 1))
                else:
                    dve.wait_ge(misc_taken, st.at(lambda t: misc_through(t, "out_proj")))

            def norm_stats(st, k, lag):
                if st.live(lag):
                    for tile in range(NT):
                        dve.bn_stats(stats[k][:, tile, :], x_rows(st, lag, tile * E, E)).then_inc(stats_done[k], 1)

            def wait_stats(st, k, lag):
                if st.live(lag):
                    dve.wait_ge(stats_done[k], st.at(lambda t: 2 * (t - lag + 1)))

            def norm_mean(st, k, lag):
                if st.live(lag):
                    for tile in range(NT):
                        dve.bn_aggr(mv[k][:, tile, :], stats[k][:, tile, :]).then_inc(mean_done[k], 1)

            def norm_var(st, k, lag):
                if st.live(lag):
                    dve.wait_ge(mean_done[k], st.at(lambda t: 2 * (t - lag + 1)))
                    dve.tensor_scalar(var_s[k][:, :, None], mv[k][:, :, 1:2], X_SCALE ** -2, LN_EPS * X_SCALE ** -2,
                                      ALU.mult, ALU.add).then_inc(var_done[k], 1)

            def norm_apply(st, k, lag):
                if not st.live(lag):
                    return
                dve.wait_ge(rstd_done[k], st.at(lambda t: t - lag + 1))
                for tile in range(NT):
                    a = dve.tensor_scalar(xhat[k][:, tile, :], x_rows(st, lag, tile * E, E), mv[k][:, tile, 0:1],
                                          rstd[k][:, tile:tile + 1], ALU.subtract, ALU.mult)
                a.then_inc(xhat_done[k], 1)

            def add_residual(st, src, scale, lag, done):
                rows = x_rows(st, lag)
                return dve.scalar_tensor_tensor(out=rows, in0=src[:, :], scalar=scale[:, :], in1=x_rows(st, lag),
                                                op0=ALU.mult, op1=ALU.add).then_inc(done, 1)

            def ffn_added(st, s):
                lag, done = {1: (4, ffn2_added), 5: (0, ffn1_added)}[s]
                if not st.live(lag):
                    return
                dve.wait_ge(down_done, st.at(lambda t: rounds_before(t, s - 1)))
                add_residual(st, down_ps, down_scale, lag, done)

            def low_part(st, lag, dst, high, hi_done):
                dve.wait_ge(hi_done, st.at(lambda t: t - lag + 1))
                dve.tensor_tensor(dst[:, :, :].rearrange("p c n -> p (c n)"), misc_ps[:, :],
                                  high[:, :, :].rearrange("p c n -> p (c n)"), ALU.subtract).then_inc(misc_taken, 1)

            def misc(st, s, place):
                for name, lag in misc_uses(s, place):
                    if not st.live(lag):
                        continue
                    if name.startswith("norm"):
                        k = int(name[-1])
                        low_part(st, lag, xt_lo[k], xt_hi[k], xt_hi_done[k])
                    elif name == "attn_t":
                        low_part(st, lag, attn_l, attn_h, attn_h_done)
                    elif name in STACK_DVE:
                        copy_stack(dve, st, name, lag, dve.tensor_copy)
                    elif name == "v":
                        v = v_row[:, (st.first - lag) % 2, :, :]
                        dve.wait_ge(v_hi_done, st.at(lambda t: t - lag + 1))
                        dve.scalar_tensor_tensor(out=v[:, :, HD:2 * HD],
                                                 in0=misc_ps[:, :].rearrange("p (m d) -> p m d", d=HD),
                                                 scalar=QKV_OUT, in1=v[:, :, 0:HD], op0=ALU.mult,
                                                 op1=ALU.subtract).then_inc(misc_taken, 1)
                    elif name == "out_proj":
                        dve.wait_ge(misc_written, st.at(lambda t: misc_through(t, name)))
                        add_residual(st, misc_ps, proj_scale, lag, misc_taken)

            def row_max(st, s):
                dve.wait_ge(scores_done, st.at(lambda t: SLOTS * (t - 2) + s + 1))
                dve.tensor_reduce(neg_max[:, 0:2], score_ps[:, :, 0:256], AX.X, ALU.max, negate=True)
                dve.tensor_reduce(neg_max[:, 2:4], score_ps[:, :, 256:384], AX.X, ALU.max, negate=True
                                  ).then_inc(max_done, 1)

            def exp_biases(st, s):
                dve.wait_ge(max_done, st.at(lambda t: SLOTS * (t - 2) + s + 1))
                dve.tensor_scalar(exp_bias[:, :], neg_max[:, :], exp_scale[:, :], None, ALU.mult
                                  ).then_inc(bias_done, 1)

            def pv_parts(s):
                return (2, s - 2) if s >= 2 else (3, s - 2 + SLOTS)

            pv = pv_ps[:, 0:4 * VW].rearrange("p (n j w) -> p n j w", n=NT, j=2)

            def pv_inverse(st, s):
                lag, pair = pv_parts(s)
                if st.live(lag):
                    dve.wait_ge(pv_done, st.at(lambda t: SLOTS * (t - lag) + pair + 1))
                    dve.reciprocal(inv_sum[:, :, :, :], pv[:, :, :, 2 * HD:VW]).then_inc(inv_done, 1)

            def pv_add(st, s):
                lag, pair = pv_parts(s)
                if st.live(lag):
                    dve.wait_ge(pv_done, st.at(lambda t: SLOTS * (t - lag) + pair + 1))
                    dve.tensor_reduce(pv_sum[:, :, :, :].rearrange("p n j d -> p (n j) d"),
                                      pv_ps[:, 0:4 * VW].rearrange("p (m w) -> p m w", w=VW)[:, :, 0:2 * HD]
                                      .rearrange("p m (a d) -> p m d a", a=2), AX.X, ALU.add
                                      ).then_inc(pv_sum_done, 1)

            def pv_scale(st, s):
                lag, pair = pv_parts(s)
                if st.live(lag):
                    if pair == 0:
                        dve.wait_ge(attn_h_done, st.at(lambda t: t - lag))
                    dve.wait_ge(inv_done, st.at(lambda t: SLOTS * (t - lag) + pair + 1))
                    dve.wait_ge(pv_sum_done, st.at(lambda t: SLOTS * (t - lag) + pair + 1))
                    dve.tensor_tensor(attn[:, :, 2 * pair * HD:2 * (pair + 1) * HD]
                                      .rearrange("p n (j d) -> p n j d", j=2), pv_sum[:, :, :, :],
                                      inv_sum[:, :, :, :].to_broadcast([P, NT, 2, HD]), ALU.mult
                                      ).then_inc(attn_done, 1)

            def prob_lo_1(st, s):
                lag, pair = (2, s - 1) if s else (3, SLOTS - 1)
                if not st.live(lag):
                    return
                dve.wait_ge(prob_h_done, st.at(lambda t: 2 * (SLOTS * (t - lag) + pair + 1)))
                dve.tensor_tensor(prob_l[:, pair % 2, 1, :], probt_ps[:, 0:384], prob_h[:, pair % 2, 1, :],
                                  ALU.subtract).then_inc(prob_l_done[1], 1)

            def silu(st, s):
                if not st.live(0 if s < ROUNDS else 3):
                    return
                dve.wait_ge(tanh_done, st.at(lambda t: rounds_before(t, s) + 1))
                dve.scalar_tensor_tensor(out=silu_b[:, :], in0=tanh_b[:, :], scalar=1.0, in1=up_ps[:, :],
                                         op0=ALU.add, op1=ALU.mult).then_inc(silu_done, 1)

            def hidden(st, s):
                if not st.live(0 if s < ROUNDS else 3):
                    return
                dve.wait_ge(hid_l_done, st.at(lambda t: rounds_before(t, s) - 1))
                dve.wait_ge(gate_done, st.at(lambda t: rounds_before(t, s) + 1))
                dve.wait_ge(silu_done, st.at(lambda t: rounds_before(t, s) + 1))
                dve.scalar_tensor_tensor(out=hid[:, s % 2, :], in0=silu_b[:, :], scalar=0.25 / X_SCALE ** 2,
                                         in1=gate_ps[:, :], op0=ALU.mult, op1=ALU.mult).then_inc(hid_done, 1)

            lag_of_norm = {1: -1, 2: 0, 3: 3}
            norm_parts = {"rows": wait_norm_rows, "stats": norm_stats, "stats_wait": wait_stats, "mean": norm_mean,
                          "var": norm_var, "apply": norm_apply}
            parts = {"pv_inverse": pv_inverse, "pv_add": pv_add, "pv_scale": pv_scale, "silu": silu, "hidden": hidden}

            def step(st):
                for s in range(SLOTS):
                    for what in DVE_OTHER.get(s, DVE_SLOT):
                        for extra in DVE_EXTRA.get((s, what), []):
                            if extra == "ffn_added":
                                ffn_added(st, s)
                            elif extra.startswith("lo"):
                                row_lo(dve, st, int(extra[-2]), int(extra[-1]))
                            else:
                                k = int(extra[-1])
                                norm_parts[extra[:-2]](st, k, lag_of_norm[k])
                        if what in parts:
                            parts[what](st, s)
                        elif what.startswith("misc"):
                            misc(st, s, what[-1])
                        elif what.startswith("prob_lo_1"):
                            prob_lo_1(st, s)
                        elif what == "row_max" and st.live(2):
                            row_max(st, s)
                        elif what == "exp_biases" and st.live(2):
                            exp_biases(st, s)
                    if st.first == 0 and s < ROUNDS:
                        (weight_maxima, weight_powers, split_weights_hi, split_weights_lo)[s]()

            set_up_constants()
            run_steps(dve, step, before={0: set_up_ternary, 1: set_up_casts})

        @block.gpsimd
        def _(pool):
            def rstd_power(st, k, lag):
                if not st.live(lag):
                    return
                pool.wait_ge(var_done[k], st.at(lambda t: t - lag + 1))
                pool.tensor_tensor(rstd[k][:, :], var_s[k][:, :], minus_half[:, :], ALU.pow).then_inc(rstd_done[k], 1)

            def norm_apply(st, k, lag):
                if not st.live(lag):
                    return
                rows = x_rows(st, lag).rearrange("p (n e) -> p n e", n=NT)
                pool.tensor_tensor(centred[k][:, :, :], rows, mv[k][:, :, 0:1].to_broadcast([P, NT, E]), ALU.subtract
                                   ).then_inc(centred_done[k], 1)
                pool.wait_ge(centred_done[k], st.at(lambda t: t - lag + 1))
                pool.wait_ge(rstd_done[k], st.at(lambda t: t - lag + 1))
                pool.tensor_tensor(xhat[k][:, :, :], centred[k][:, :, :], rstd[k][:, :, None].to_broadcast([P, NT, E]),
                                   ALU.mult).then_inc(xhat_done[k], 1)

            def rope_mul(st, tile):
                if not st.live(1):
                    return
                if st.first == 1 and tile == 0:
                    pool.wait_ge(rope_loaded, 32)
                pool.wait_ge(misc_taken, st.at(lambda t: misc_through(t, f"qk{tile}")))
                pool.tensor_tensor(rope_c[:, tile, :], qk_rows[:, tile, :], cos[:, tile, :], ALU.mult)
                pool.tensor_tensor(rope_s[:, tile, :], qk_rows[:, tile, :], sin[:, tile, :], ALU.mult
                                   ).then_inc(rope_mul_done, 1)

            def rope_add(st, tile):
                if not st.live(1):
                    return
                pool.wait_ge(rope_mul_done, st.at(lambda t: 2 * (t - 1) + tile + 1))

                def halves(a):
                    return a[:, tile, :].rearrange("p (h a d) -> p h a d", a=2, d=HD // 2)

                pool.tensor_tensor(halves(rope_r), halves(rope_c), halves(rope_s)[:, :, ::-1, :], ALU.add
                                   ).then_inc(rope_done, 1)

            def prob_lo_0(st, s):
                lag, pair = (2, s - 1) if s else (3, SLOTS - 1)
                if not st.live(lag):
                    return
                pool.wait_ge(prob_t_done, st.at(lambda t: SLOTS * (t - lag) + pair + 1))
                pool.tensor_tensor(prob_l[:, pair % 2, 0, :], prob_t[:, pair % 2, :], prob_h[:, pair % 2, 0, :],
                                   ALU.subtract).then_inc(prob_l_done[0], 1)

            def hidden_lo(st, s):
                if not st.live(0 if s < ROUNDS else 3):
                    return
                pool.wait_ge(hid_h_done, st.at(lambda t: rounds_before(t, s) + 1))
                pool.tensor_tensor(hid_l[:, s % 2, :, :].rearrange("p m n -> p (m n)"), hid[:, s % 2, :],
                                   hid_h[:, s % 2, :, :].rearrange("p m n -> p (m n)"), ALU.subtract
                                   ).then_inc(hid_l_done, 1)

            def step(st):
                lag_of_norm = {1: -1, 2: 0, 3: 3}
                for s in range(SLOTS):
                    if st.first == 0 and s == 1:
                        max_all()
                    for what in POOL_SLOT[s]:
                        if what == "hidden_lo":
                            hidden_lo(st, s)
                        elif what == "prob_lo":
                            prob_lo_0(st, s)
                        elif what.startswith("mul"):
                            rope_mul(st, int(what[-1]))
                        elif what.startswith("add"):
                            rope_add(st, int(what[-1]))
                        elif what.startswith("lo"):
                            row_lo(pool, st, int(what[-2]), int(what[-1]))
                        elif what.startswith("pow"):
                            rstd_power(st, int(what[-1]), lag_of_norm[int(what[-1])])
                        elif what.startswith("apply"):
                            norm_apply(st, int(what[-1]), lag_of_norm[int(what[-1])])

            def sum_all():
                pool.wait_ge(abs_done, 2)
                pool.partition_all_reduce(abs_sum_all[:, 0:2], abs_sum[:, 0:2], P, RADD).then_inc(abs_all, 1)
                pool.wait_ge(abs_done, 3)
                pool.partition_all_reduce(abs_sum_all[:, 2:3], abs_sum[:, 2:3], P, RADD).then_inc(abs_all, 1)

            def max_all():
                pool.wait_ge(wmax_done, 1)
                pool.partition_all_reduce(w_max_all[:, :], w_max[:, :], P, RMAX).then_inc(wmax_all, 1)

            pool.wait_ge(casts_done, 1)
            run_steps(pool, step, before={0: sum_all})


def kernel(L0_attn_x, L0_attn_wq, L0_attn_wk, L0_attn_wv, L0_attn_wo, L0_ffn_W_up, L0_ffn_W_gate, L0_ffn_W_down):
    import concourse.bacc as bacc
    from concourse.bass_utils import run_bass_kernel_spmd

    def rows_to_partitions(a):
        a = np.ascontiguousarray(a)
        return np.ascontiguousarray(a.reshape(a.shape[0] // P, P, a.shape[1]).transpose(1, 0, 2).reshape(P, -1))

    wqkvo = np.stack([rows_to_partitions(w).reshape(P, NC, E)
                      for w in (L0_attn_wq, L0_attn_wk, L0_attn_wv, L0_attn_wo)], axis=2)

    freq = (1.0 / np.float32(10000.0) ** (np.arange(0, HD, 2, dtype=np.float32) / np.float32(HD))).astype(np.float32)
    angle = np.arange(SEQ, dtype=np.float32)[:, None] * freq[None, :]
    s, c = np.sin(angle) * np.float32(QKV_OUT), np.cos(angle) * np.float32(QKV_OUT)

    def table(first_half, second_half):
        head = np.concatenate([first_half, second_half], axis=1).astype(np.float32)
        return np.ascontiguousarray(np.tile(head, (1, 2 * HEADS)).reshape(NT, P, 2 * E).transpose(1, 0, 2))

    future = np.triu(np.full((P, P), MASKED, dtype=np.float32), k=1)
    arrays = {
        "x": np.ascontiguousarray(L0_attn_x),
        "wqkvo": np.ascontiguousarray(wqkvo),
        "w_up_t": rows_to_partitions(np.asarray(L0_ffn_W_up).T),
        "w_gate_t": rows_to_partitions(np.asarray(L0_ffn_W_gate).T),
        "w_down_t": rows_to_partitions(np.asarray(L0_ffn_W_down).T),
        "ident": np.eye(P, dtype=np.float32),
        "mask": np.concatenate([future, future], axis=1),
        "rope_cos": table(c, c),
        "rope_sin": table(s, -s),
    }
    nc = bacc.Bacc("TRN2", target_bir_lowering=False, num_devices=1)
    args = [nc.dram_tensor(n, a.shape, mybir.dt.from_np(a.dtype), kind="ExternalInput").ap() for n, a in arrays.items()]
    out = nc.dram_tensor("out", (NBATCH, SEQ, E), F32, kind="ExternalOutput").ap()
    macaron_kernel(nc, *args, out)
    return run_bass_kernel_spmd(nc, [arrays], core_ids=[0]).results[0]["out"]
```
